# Optimizing a Trainium2 kernel written in Bass

```python
import numpy as np
import jax
import jax.numpy as jnp

def _softmax(x, axis=-1):
    return jax.nn.softmax(x, axis=axis)

def _gelu(x):
    return jax.nn.gelu(x, approximate=True)

def _silu(x):
    return jax.nn.silu(x)

def _sigmoid(x):
    return jax.nn.sigmoid(x)

def _layernorm(x, axis=-1, eps=1e-05):
    m = jnp.mean(x, axis=axis, keepdims=True)
    v = jnp.var(x, axis=axis, keepdims=True)
    return (x - m) / jnp.sqrt(v + eps)

def _scatter_add(tgt, idx, src, axis=0):
    return tgt.at[idx].add(src)

def _segment_sum(src, seg, n):
    return jax.ops.segment_sum(src, seg, n)
kernel_name = 'mk_conv_attn_hybrid_d2_conv_nchw512_r2_d289b2'

def setup_inputs(seed: int=0):
    np.random.seed(seed)
    _w = jnp.asarray

    def _rec_inputs():
        import jax
        import jax.numpy as jnp
        _gk = jax.random.key(seed)
        x = -0.0002928 + 1 * jax.random.normal(jax.random.fold_in(_gk, 1), (8, 256, 32, 32), jnp.float32)
        return x
    x = _rec_inputs()

    def _L0_conv_setup():
        import jax, jax.numpy as jnp
        import numpy as np
        import math
        GROUPS = 32
        EPS = 1e-05
        N_HEADS = 8

        def group_norm(x, w, b):
            B, C, T = x.shape
            xg = x.reshape(B, GROUPS, C // GROUPS * T)
            mu = xg.mean(axis=-1, keepdims=True)
            var = xg.var(axis=-1, keepdims=True)
            xn = ((xg - mu) * jax.lax.rsqrt(var + EPS)).reshape(B, C, T)
            return xn * w[None, :, None] + b[None, :, None]
        key = jax.random.key(seed)
        ks = jax.random.split(key, 7)
        C = 256
        return {'x': jax.random.normal(ks[0], (8, C, 32, 32), dtype=jnp.float32), 'norm_w': jax.random.normal(ks[1], (C,), dtype=jnp.float32), 'norm_b': jax.random.normal(ks[2], (C,), dtype=jnp.float32), 'qkv_w': jax.random.normal(ks[3], (3 * C, C), dtype=jnp.float32) * 0.02, 'qkv_b': jax.random.normal(ks[4], (3 * C,), dtype=jnp.float32) * 0.02, 'proj_w': jax.random.normal(ks[5], (C, C), dtype=jnp.float32) * 0.02, 'proj_b': jax.random.normal(ks[6], (C,), dtype=jnp.float32) * 0.02}
    _L0_conv_all = _L0_conv_setup()
    _L0_conv_in = {k: v for k, v in _L0_conv_all.items() if k in ('norm_w', 'norm_b', 'qkv_w', 'qkv_b', 'proj_w', 'proj_b')}
    del _L0_conv_all

    def _L1_attn_setup():
        import math
        import jax, jax.numpy as jnp
        import numpy as np
        NUM_HEADS = 8
        key = jax.random.key(seed)
        ks = jax.random.split(key, 6)
        B, T, D = (2, 2048, 256)
        scale = 1.0 / math.sqrt(D)
        return {'combined_embed': jax.random.normal(ks[0], (B, T, D), dtype=jnp.float32), 'W_K': jax.random.normal(ks[1], (D, D), dtype=jnp.float32) * scale, 'b_K': jnp.zeros((D,), dtype=jnp.float32), 'W_Q': jax.random.normal(ks[2], (D, D), dtype=jnp.float32) * scale, 'b_Q': jnp.zeros((D,), dtype=jnp.float32), 'W_V': jax.random.normal(ks[3], (D, D), dtype=jnp.float32) * scale, 'b_V': jnp.zeros((D,), dtype=jnp.float32), 'W_O': jax.random.normal(ks[4], (D, D), dtype=jnp.float32) * scale, 'b_O': jnp.zeros((D,), dtype=jnp.float32)}
    _L1_attn_all = _L1_attn_setup()
    _L1_attn_in = {k: v for k, v in _L1_attn_all.items() if k in ('W_K', 'b_K', 'W_Q', 'b_Q', 'W_V', 'b_V', 'W_O', 'b_O')}
    del _L1_attn_all

    def _L1_ffn_setup():
        import jax, jax.numpy as jnp
        import numpy as np
        TOP_K = 2
        key = jax.random.key(seed)
        k1, k2, k3, k4 = jax.random.split(key, 4)
        B, S, d = (4, 1024, 256)
        E, H = (32, 64)
        x = jax.random.normal(k1, (B, S, d), dtype=jnp.float32)
        expert_sel = jax.random.normal(k2, (E, d), dtype=jnp.float32) / np.sqrt(d).astype(np.float32)
        keys = jax.random.normal(k3, (E, d, H), dtype=jnp.float32) / np.sqrt(d).astype(np.float32)
        values = jax.random.normal(k4, (E, H, d), dtype=jnp.float32) / np.sqrt(E * H).astype(np.float32)
        return {'x': x, 'expert_sel': expert_sel, 'keys': keys, 'values': values}
    _L1_ffn_all = _L1_ffn_setup()
    _L1_ffn_in = {k: v for k, v in _L1_ffn_all.items() if k in ('expert_sel', 'keys', 'values')}
    del _L1_ffn_all
    return {'x': x, 'L0_conv_norm_w': _L0_conv_in['norm_w'], 'L0_conv_norm_b': _L0_conv_in['norm_b'], 'L0_conv_qkv_w': _L0_conv_in['qkv_w'], 'L0_conv_qkv_b': _L0_conv_in['qkv_b'], 'L0_conv_proj_w': _L0_conv_in['proj_w'], 'L0_conv_proj_b': _L0_conv_in['proj_b'], 'L1_attn_W_K': _L1_attn_in['W_K'], 'L1_attn_b_K': _L1_attn_in['b_K'], 'L1_attn_W_Q': _L1_attn_in['W_Q'], 'L1_attn_b_Q': _L1_attn_in['b_Q'], 'L1_attn_W_V': _L1_attn_in['W_V'], 'L1_attn_b_V': _L1_attn_in['b_V'], 'L1_attn_W_O': _L1_attn_in['W_O'], 'L1_attn_b_O': _L1_attn_in['b_O'], 'L1_ffn_expert_sel': _L1_ffn_in['expert_sel'], 'L1_ffn_keys': _L1_ffn_in['keys'], 'L1_ffn_values': _L1_ffn_in['values']}

def reference(x, L0_conv_norm_w, L0_conv_norm_b, L0_conv_qkv_w, L0_conv_qkv_b, L0_conv_proj_w, L0_conv_proj_b, L1_attn_W_K, L1_attn_b_K, L1_attn_W_Q, L1_attn_b_Q, L1_attn_W_V, L1_attn_b_V, L1_attn_W_O, L1_attn_b_O, L1_ffn_expert_sel, L1_ffn_keys, L1_ffn_values):
    import jax
    import jax.numpy as jnp

    def _L0_conv_ref(x, norm_w, norm_b, qkv_w, qkv_b, proj_w, proj_b):
        import jax, jax.numpy as jnp
        import numpy as np
        import math
        GROUPS = 32
        EPS = 1e-05
        N_HEADS = 8

        def group_norm(x, w, b):
            B, C, T = x.shape
            xg = x.reshape(B, GROUPS, C // GROUPS * T)
            mu = xg.mean(axis=-1, keepdims=True)
            var = xg.var(axis=-1, keepdims=True)
            xn = ((xg - mu) * jax.lax.rsqrt(var + EPS)).reshape(B, C, T)
            return xn * w[None, :, None] + b[None, :, None]
        b, c, H, W = x.shape
        T = H * W
        xf = x.reshape(b, c, T)
        xn = group_norm(xf, norm_w, norm_b)
        qkv = jnp.einsum('oc,bct->bot', qkv_w, xn) + qkv_b[None, :, None]
        ch = c // N_HEADS
        qkv = qkv.reshape(b * N_HEADS, 3 * ch, T)
        q, k, v = (qkv[:, :ch], qkv[:, ch:2 * ch], qkv[:, 2 * ch:])
        scale = 1.0 / math.sqrt(math.sqrt(ch))
        weight = jnp.einsum('bct,bcs->bts', q * scale, k * scale)
        weight = jax.nn.softmax(weight.astype(jnp.float32), axis=-1).astype(qkv.dtype)
        a = jnp.einsum('bts,bcs->bct', weight, v).reshape(b, c, T)
        hout = jnp.einsum('oc,bct->bot', proj_w, a) + proj_b[None, :, None]
        return (xf + hout).reshape(b, c, H, W)

    def _L1_attn_ref(combined_embed, W_K, b_K, W_Q, b_Q, W_V, b_V, W_O, b_O):
        import math
        import jax, jax.numpy as jnp
        import numpy as np
        NUM_HEADS = 8
        B, T, D = combined_embed.shape
        H = NUM_HEADS
        hd = D // H
        K = combined_embed @ W_K + b_K
        Q = combined_embed @ W_Q + b_Q
        V = combined_embed @ W_V + b_V
        K = K.reshape(B, T, H, hd).transpose(0, 2, 1, 3)
        Q = Q.reshape(B, T, H, hd).transpose(0, 2, 1, 3)
        V = V.reshape(B, T, H, hd).transpose(0, 2, 1, 3)
        scores = jnp.einsum('bhqd,bhkd->bhqk', Q, K) / jnp.sqrt(jnp.float32(hd))
        causal = jnp.tril(jnp.ones((T, T), dtype=bool))
        scores = jnp.where(causal, scores, -jnp.inf)
        W = jax.nn.softmax(scores, axis=-1)
        Z = jnp.einsum('bhqk,bhkd->bhqd', W, V)
        Z = Z.transpose(0, 2, 1, 3).reshape(B, T, D)
        return Z @ W_O + b_O

    def _L1_ffn_ref(x, expert_sel, keys, values):
        import jax, jax.numpy as jnp
        import numpy as np
        TOP_K = 2
        B, S, d = x.shape
        E = keys.shape[0]
        xt = x.reshape(-1, d)
        T = xt.shape[0]
        sel = jax.nn.sigmoid(xt @ expert_sel.T)
        sel_val, sel_idx = jax.lax.top_k(sel, TOP_K)
        w = jnp.zeros((T, E), dtype=xt.dtype).at[jnp.arange(T)[:, None], sel_idx].add(sel_val)
        h = jax.nn.relu(jnp.einsum('td,edh->teh', xt, keys))
        out = jnp.einsum('teh,te,ehv->tv', h, w, values)
        return out.reshape(B, S, -1)

    def _gn(v, G=32, eps=1e-05):
        B_, C_, H_, W_ = v.shape
        g = v.reshape(B_, G, C_ // G, H_, W_)
        m = jnp.mean(g, axis=(2, 3, 4), keepdims=True)
        s = jnp.var(g, axis=(2, 3, 4), keepdims=True)
        return ((g - m) / jnp.sqrt(s + eps)).reshape(v.shape)

    def _ln_c(v, eps=1e-06):
        m = jnp.mean(v, axis=1, keepdims=True)
        s = jnp.var(v, axis=1, keepdims=True)
        return (v - m) / jnp.sqrt(s + eps)

    def _ln_t(v, eps=1e-05):
        m = jnp.mean(v, axis=-1, keepdims=True)
        s = jnp.var(v, axis=-1, keepdims=True)
        return (v - m) / jnp.sqrt(s + eps)

    def _to_tokens(v):
        B_, C_, H_, W_ = v.shape
        return v.reshape(B_, C_, H_ * W_).transpose(0, 2, 1)

    def _from_tokens(t, like):
        B_, C_, H_, W_ = like.shape
        return t.transpose(0, 2, 1).reshape(B_, C_, H_, W_)
    x = _L0_conv_ref(x, L0_conv_norm_w, L0_conv_norm_b, L0_conv_qkv_w, L0_conv_qkv_b, L0_conv_proj_w, L0_conv_proj_b)
    t = _to_tokens(x)
    t = t + _L1_attn_ref(_ln_t(t), L1_attn_W_K, L1_attn_b_K, L1_attn_W_Q, L1_attn_b_Q, L1_attn_W_V, L1_attn_b_V, L1_attn_W_O, L1_attn_b_O)
    t = t + _L1_ffn_ref(_ln_t(t), L1_ffn_expert_sel, L1_ffn_keys, L1_ffn_values)
    x = _from_tokens(t, x)
    return x

_drawn_inputs = setup_inputs


def setup_inputs(seed=0):
    import zlib

    import numpy as np

    out = dict(_drawn_inputs(seed))
    spreads = {'L1_attn_b_K': (0.0, 0.8),
     'L1_attn_b_Q': (0.0, 0.323),
     'L1_attn_b_V': (0.0, 0.1),
     'L1_attn_b_O': (0.0, 0.1)}
    factors = {'L0_conv_norm_w': 4.803, 'L0_conv_qkv_b': 3.424}
    for name, (base, spread) in spreads.items():
        noise = np.random.default_rng([zlib.crc32(name.encode()), seed]).standard_normal(out[name].shape)
        drawn = base * np.exp(spread * noise) if base else spread * noise
        out[name] = jnp.asarray(drawn.astype(out[name].dtype))
    for name, factor in factors.items():
        out[name] = (out[name] * factor).astype(out[name].dtype)
    return out
```

```python
from contextlib import ExitStack

import numpy as np

import concourse.bass as bass
from concourse import mybir

ACT = mybir.ActivationFunctionType
ALU = mybir.AluOpType
AX_X = mybir.AxisListType.X
F32 = mybir.dt.float32
F32R = mybir.dt.float32r
BF16 = mybir.dt.bfloat16

P = 128
HALF = 512
HEADS_PER_GROUP = 4
MASKED = -1.0e30


def numbered(keys):
    return {key: n + 1 for n, key in enumerate(keys)}


def merged(main, side, every, after=0):
    out, side = [], list(side)
    for n, step in enumerate(main):
        out.append(step)
        if n >= after and (n - after) % every == every - 1 and side:
            out.append(side.pop(0))
    return out + side


def spread(main, side):
    out, done = [], 0
    for n, step in enumerate(main):
        out.append(step)
        upto = len(side) * (n + 1) // len(main)
        out += side[done:upto]
        done = upto
    return out


def attention_steps(stage, tiles, halves):
    per_half = tiles // halves

    def qk(g):
        return [("qk", stage, g, w, hf) for w in "qk" for hf in range(halves)]

    def top(g):
        out = []
        for j in range(HEADS_PER_GROUP):
            out += [("top", stage, g, j, i) for i in range(tiles)] + [("row", stage, g, j)]
        return out

    def mix(g):
        out = []
        for hf in range(halves):
            last = per_half * (hf + 1) if stage else tiles
            out += [("mix", stage, g, hf, k) for k in range(last)] + [("norm", stage, g, hf)]
        return out

    steps = qk(0) + [("v", stage, n) for n in range(tiles // 2)]
    steps += merged(top(0), qk(1), 3, 2)
    steps += spread(mix(0), top(1))
    steps += mix(1)
    return steps


def bass_hybrid_kernel(nc: bass.Bass, x, mats, vecs, norm_wb, sel_t, keys_t, values, out, w_dram):
    B, C, T = x.shape
    E = sel_t.shape[2]
    H = values.shape[0] // E
    CT = C // P
    NH = T // HALF
    TT = T // P
    PH = HALF // P
    G = HEADS_PER_GROUP
    HD = P // G
    MID = 3 * HD
    ET = E * H // P
    EPT = P // H
    RING = 4
    SCALE = float(HD) ** -0.5
    NORM_GROUP = C // 32

    ATT = [attention_steps(st, TT, NH) for st in range(2)]
    LNH = [(ln, hf) for ln in range(2) for hf in range(NH)]
    OUTS = [(st, hf, ct) for st in range(2) for hf in range(NH) for ct in range(CT)]
    MOE = [(j, hf) for j in range(ET) for hf in range(NH)]

    STEPS = [("gn",)] + ATT[0] + [("out", 0, hf, ct) for hf in range(NH) for ct in range(CT)]
    STEPS += [("ln", 0, hf) for hf in range(NH)] + ATT[1]
    STEPS += [("out", 1, hf, ct) for hf in range(NH) for ct in range(CT)]
    STEPS += [("ln", 1, hf) for hf in range(NH)] + [("route",)]
    STEPS += [("up", j, hf) for j, hf in MOE] + [("down",)] + [("end",)]

    def cols(st, i):
        return P * (i + 1) if st else T

    def first(st, hf, k):
        return max(0, P * (k - PH * hf)) if st else 0

    single = []
    double = []
    for s in STEPS:
        if s[0] in ("qk", "v", "out"):
            single.append(s)
        elif s[0] == "mix":
            single += [s + (j,) for j in range(G)]
        elif s[0] == "ln":
            single += [s + ("mean",), s + ("var",)]
        elif s[0] == "up":
            single.append(s)
        elif s[0] in ("top", "row"):
            double.append(s)
    s_slot = {u: n % 2 for n, u in enumerate(single)}
    s_use = {u: n // 2 + 1 for n, u in enumerate(single)}
    s_uses = [len(single) - len(single) // 2, len(single) // 2]
    d_slot = {u: n % 2 for n, u in enumerate(double)}
    d_use = {u: n // 2 + 1 for n, u in enumerate(double)}
    d_uses = [len(double) - len(double) // 2, len(double) // 2]

    of = {}
    for s in STEPS:
        of.setdefault(s[0], []).append(s)
    mix_no = numbered(of["mix"])
    norm_no = numbered(of["norm"])
    row_no = numbered(of["row"])
    qk_no = numbered(of["qk"])
    v_no = numbered(of["v"])
    out_no = numbered(of["out"])
    ln_no = numbered(of["ln"])
    n_mix, n_norm, n_row, n_qk, n_v = (len(of[k]) for k in ("mix", "norm", "row", "qk", "v"))
    n_out, n_ln, n_up = len(of["out"]), len(of["ln"]), len(MOE)
    group_no = numbered([(st, g) for st in range(2) for g in range(CT)])
    n_group = len(group_no)
    n_stack_dma = 6 * G

    with ExitStack() as ctx:
        def sb(name, shape, dt=F32):
            return ctx.enter_context(nc.sbuf_tensor(name, shape, dt))

        def sem(name):
            return ctx.enter_context(nc.semaphore(name))

        w_hi = sb("w_hi", [P, 8, CT, C], F32R)
        w_lo = sb("w_lo", [P, 8, CT, C], F32R)
        bias = sb("bias", [P, 8, CT])
        gnw = sb("gnw", [P, 2, CT])
        sel_w = sb("sel_w", [P, CT, E])
        ident = sb("ident", [P, P])
        ident_bf = sb("ident_bf", [P, P], BF16)
        minus_bf = sb("minus_bf", [P, P], BF16)
        mask_qk = sb("mask_qk", [P, P], BF16)
        mask_kq = sb("mask_kq", [P, P], BF16)
        mean_w = sb("mean_w", [P, P])
        block_w = sb("block_w", [P, P])
        ones32 = sb("ones32", [P, HD])

        x_in = sb("x_in", [P, CT, T])
        x_res = sb("x_res", [P, CT, T])
        xn = sb("xn", [P, CT, T])
        act_hi = sb("act_hi", [P, CT, T], F32R)
        act_lo = sb("act_lo", [P, CT, T], F32R)
        nat_hi = sb("nat_hi", [P, 2, T], F32R)
        nat_lo = sb("nat_lo", [P, 2, T], F32R)
        q_st = sb("q_st", [P, CT, G, T], F32R)
        k_st = sb("k_st", [P, CT, G, T], F32R)
        v_sb = sb("v_sb", [P, TT, C])
        probs = sb("probs", [P, 2, G, HALF])
        tops = sb("tops", [P, G, TT], BF16)
        rsum = sb("rsum", [P, HALF])
        var_sb = sb("var_sb", [P, HALF])
        rstd = sb("rstd", [P, HALF])
        st6 = sb("st6", [P, CT, NH, 6])
        mv = sb("mv", [P, CT, 2])
        small = sb("small", [P, 8, CT, 2])
        keys_sb = sb("keys_sb", [P, RING, CT, P])
        vals_sb = sb("vals_sb", [P, RING, C])
        pad_sel = sb("pad_sel", [P, TT, E + 8])
        rest = sb("rest", [P, TT, E + 8])
        top8 = sb("top8", [P, TT, 8])
        w_tok = sb("w_tok", [P, TT, E])
        w_turn = sb("w_turn", [P, NH, P])
        gated = probs[:, 0, :, :]
        gate_bc = probs[:, 1, :, :].rearrange("p g t -> p (g t)").rearrange("p (r t) -> p r t", t=T)

        ps_top = ctx.enter_context(nc.psum_tensor("ps_top", [P, 2, T], F32))
        ps_one = ctx.enter_context(nc.psum_tensor("ps_one", [P, 2, HALF], F32))
        ps_o = ctx.enter_context(nc.psum_tensor("ps_o", [P, HALF], F32))
        ps_s = ctx.enter_context(nc.psum_tensor("ps_s", [P, HALF], F32))

        passed = sem("passed")
        consts = sem("consts")
        fills = sem("fills")
        weights_in = sem("weights_in")
        weights_hi = sem("weights_hi")
        weights_lo = sem("weights_lo")
        x_loaded = sem("x_loaded")
        one_full = [sem(f"one_full{n}") for n in range(2)]
        one_free = [sem(f"one_free{n}") for n in range(2)]
        top_full = [sem(f"top_full{n}") for n in range(2)]
        top_free = [sem(f"top_free{n}") for n in range(2)]
        vec = sem("vec")
        gn_stats = sem("gn_stats")
        gn_means = sem("gn_means")
        gn_var = sem("gn_var")
        gn_rstd = sem("gn_rstd")
        logged = sem("logged")
        xn_ready = sem("xn_ready")
        hi_ready = sem("hi_ready")
        lo_ready = sem("lo_ready")
        nat_hi_ready = sem("nat_hi_ready")
        nat_lo_ready = sem("nat_lo_ready")
        stacked = [sem(f"stacked{g}") for g in range(CT)]
        v_ready = sem("v_ready")
        top_ready = sem("top_ready")
        row_ready = sem("row_ready")
        mixed = sem("mixed")
        norm_done = sem("norm_done")
        att_hi = sem("att_hi")
        att_lo = sem("att_lo")
        x_res_ready = sem("x_res_ready")
        centred = sem("centred")
        squared = sem("squared")
        var_ready = sem("var_ready")
        rstd_ready = sem("rstd_ready")
        logits = sem("logits")
        sel_exp = sem("sel_exp")
        gates = sem("gates")
        turned = sem("turned")
        turned_sb = sem("turned_sb")
        gates_out = sem("gates_out")
        gate_in = [sem(f"gate_in{n}") for n in range(2)]
        expert_in = [sem(f"expert_in{n}") for n in range(RING)]
        downed = sem("downed")
        batch_over = sem("batch_over")
        store_over = sem("store_over")
        result = sem("result")
        stored = sem("stored")

        def split(pe, acc, lhs, rhs, start, stop, **kw):
            (lh, ll), (rh, rl) = lhs, rhs
            pe.matmul(acc, lh, rh, start=start, stop=False, **kw)
            pe.matmul(acc, lh, rl, start=False, stop=False, **kw)
            return pe.matmul(acc, ll, rh, start=False, stop=stop, **kw)

        def f(ap):
            return ap.bitcast(F32)

        block = ctx.enter_context(nc.Block())

        @block.sync
        def _(sp):
            sp.dma_start(probs[:, :, :, :].rearrange("p a g t -> p (a g t)"),
                         mats.rearrange("p m k c -> p (m k c)")).then_inc(weights_in, 16)
            sp.dma_start(bias[:, :, :], vecs).then_inc(weights_in, 16)
            sp.dma_start(gnw[:, :, :], norm_wb).then_inc(weights_in, 16)
            sp.dma_start(sel_w[:, :, :], sel_t).then_inc(weights_in, 16)
            sp.dma_start(x_in[:, :, :], x[0].rearrange("(k p) t -> p k t", p=P)).then_inc(x_loaded, 16)
            with sp.Fori(0, B) as it:
                def load_expert(j):
                    r = j % RING
                    sp.dma_start(keys_sb[:, r, :, :], keys_t[:, j, :, :]).then_inc(expert_in[r], 16)
                    sp.dma_start(vals_sb[:, r, :], values[P * j:P * j + P, :]).then_inc(expert_in[r], 16)

                sp.wait_ge(batch_over, it + 1)
                for j in range(RING):
                    load_expert(j)
                for s in STEPS:
                    if s[0] == "qk" and s[3:] == ("k", NH - 1):
                        _, st, g, _, _ = s
                        sp.wait_ge(nat_lo_ready, it * n_qk + qk_no[s])
                        sp.sem_inc(passed, 1)
                        if st:
                            sp.wait_ge(norm_done, it * n_norm + norm_no[("norm", 0, g, NH - 1)])
                        for j in range(G):
                            rows = slice(HD * j, HD * j + HD)
                            for stack, n, parts in ((q_st, 0, (nat_hi, nat_hi, nat_lo)),
                                                    (k_st, 1, (nat_hi, nat_lo, nat_hi))):
                                for quad, part in enumerate(parts):
                                    sp.dma_start(f(stack[HD * quad:HD * quad + HD, g, j, :]),
                                                 f(part[rows, n, :])).then_inc(stacked[g], 16)
                    if s == ("out", 0, NH - 1, CT - 1):
                        sp.wait_ge(x_res_ready, it * n_out + out_no[s])
                        ahead = nc_next(sp, it, B)
                        sp.dma_start(x_in[:, :, :], x[bass.ds(ahead, 1)].rearrange("a (k p) t -> p (a k) t", p=P)
                                     ).then_inc(x_loaded, 16)
                    if s[0] == "route":
                        sp.wait_ge(turned_sb, it + 1)
                        for hf in range(NH):
                            for i in range(PH):
                                at = (hf * PH + i) * P
                                sp.dma_start(w_dram[:, at:at + P],
                                             w_turn[E * i:E * i + E, hf, :]).then_inc(gates_out, 16)
                    if s[0] == "up" and s[2] == 0:
                        j = s[1]
                        if j == 0:
                            sp.wait_ge(gates_out, (it + 1) * 16 * TT)
                        if j >= 2:
                            for hf in range(NH):
                                u = ("up", j - 2, hf)
                                sp.wait_ge(one_free[s_slot[u]], it * s_uses[s_slot[u]] + s_use[u])
                        for e in range(EPT):
                            row = w_dram[EPT * j + e:EPT * j + e + 1, :]
                            sp.dma_start(gate_bc[H * e:H * e + H, j % 2, :],
                                         bass.AP(row.tensor, row.offset, [[0, H], [1, T]])
                                         ).then_inc(gate_in[j % 2], 16)
                    if s[0] == "up" and s[2] == NH - 1 and s[1] >= 1 and s[1] - 1 + RING < ET:
                        sp.wait_ge(downed, it * n_up + NH * s[1])
                        load_expert(s[1] - 1 + RING)
                    if s[0] == "down":
                        sp.wait_ge(result, (it + 1) * NH * CT)
                        sp.dma_start(out[bass.ds(it, 1)].rearrange("a (k p) t -> p (a k) t", p=P),
                                     x_res[:, :, :]).then_inc(stored, 16)
                        sp.wait_ge(stored, (it + 1) * 16)
                        sp.sem_inc(store_over, 1)
            sp.wait_ge(x_loaded, 16 * (B + 1))
            sp.wait_ge(gates_out, B * 16 * TT)
            sp.wait_ge(stored, B * 16)

        @block.gpsimd
        def _(pool):
            pool.memset(ident[:], 0.0).then_inc(consts, 1)
            pool.memset(ident_bf[:], 0.0).then_inc(consts, 1)
            pool.memset(minus_bf[:], 0.0).then_inc(consts, 1)
            pool.memset(mask_qk[:], 0.0).then_inc(consts, 1)
            pool.memset(mask_kq[:], 0.0).then_inc(consts, 1)
            pool.memset(block_w[:], 1.0 / NORM_GROUP).then_inc(consts, 1)
            pool.memset(mean_w[:], 1.0 / C).then_inc(consts, 1)
            pool.memset(ones32[:], 1.0).then_inc(consts, 1)
            pool.wait_ge(consts, 8)
            for m, value in ((ident, 1.0), (ident_bf, 1.0), (minus_bf, -1.0)):
                pool.affine_select(out=m[:], in_=m[:], compare_op=ALU.not_equal, fill=value, base=0,
                                   pattern=[[-1, P]], channel_multiplier=1).then_inc(consts, 1)
            pool.affine_select(out=mask_qk[:], in_=mask_qk[:], compare_op=ALU.is_ge, fill=MASKED, base=0,
                               pattern=[[-1, P]], channel_multiplier=1).then_inc(consts, 1)
            pool.affine_select(out=mask_kq[:], in_=mask_kq[:], compare_op=ALU.is_ge, fill=MASKED, base=0,
                               pattern=[[1, P]], channel_multiplier=-1).then_inc(consts, 1)
            blocks = block_w[:].rearrange("p (n e) -> p n e", e=NORM_GROUP)
            pool.affine_select(out=blocks, in_=blocks, compare_op=ALU.is_ge, fill=0.0, base=0,
                               pattern=[[-NORM_GROUP, P // NORM_GROUP], [0, NORM_GROUP]],
                               channel_multiplier=1).then_inc(consts, 1)
            pool.wait_ge(consts, 14)
            pool.affine_select(out=blocks, in_=blocks, compare_op=ALU.is_ge, fill=0.0, base=NORM_GROUP - 1,
                               pattern=[[NORM_GROUP, P // NORM_GROUP], [0, NORM_GROUP]],
                               channel_multiplier=-1).then_inc(consts, 1)

        @block.tensor
        def _(pe):
            pe.wait_ge(consts, N_CONSTS)
            pe.wait_ge(fills, 2)
            pe.wait_ge(weights_hi, 1)
            pe.wait_ge(weights_lo, 1)
            with pe.Fori(0, B) as it:
                def one(u):
                    if s_use[u] > 1:
                        pe.wait_ge(one_free[s_slot[u]], it * s_uses[s_slot[u]] + s_use[u] - 1)
                    return ps_one[:, s_slot[u], :]

                def two(u):
                    if d_use[u] > 1:
                        pe.wait_ge(top_free[d_slot[u]], it * d_uses[d_slot[u]] + d_use[u] - 1)
                    return ps_top[:, d_slot[u], :]

                def parts(m, k, lo, hi):
                    return w_hi[:, m, k, lo:hi], w_lo[:, m, k, lo:hi]

                def acts(k, lo, hi):
                    return act_hi[:, k, lo:hi], act_lo[:, k, lo:hi]

                def multiply_values(s):
                    _, st, g, hf, k = s
                    a = first(st, hf, k)
                    last = k == (PH * (hf + 1) if st else TT) - 1
                    for j in (G - 2, G - 1):
                        u = s + (j,)
                        pe.wait_ge(one_free[s_slot[u]], it * s_uses[s_slot[u]] + s_use[u])
                    if k == 0:
                        pe.wait_ge(v_ready, it * n_v + v_no[("v", st, TT // 2 - 1)])
                        n = norm_no[("norm", st, g, hf)] - 1
                        if n:
                            pe.wait_ge(norm_done, it * n_norm + n)
                    b = mix_no[s] % 2
                    for j in range(G):
                        c = P * g + HD * j
                        pe.matmul(ps_o[HD * j:HD * j + HD, a:HALF], v_sb[:, k, c:c + HD],
                                  probs[:, b, j, a:HALF], start=(k == 0), stop=last)
                    for j in range(G):
                        mm = pe.matmul(ps_s[HD * j:HD * j + HD, a:HALF], ones32[:],
                                       probs[:, b, j, a:HALF], start=(k == 0), stop=last)
                    mm.then_inc(mixed, 1)

                pe.wait_ge(batch_over, it + 1)
                for s in STEPS:
                    kind = s[0]
                    if kind == "gn":
                        pe.wait_ge(gn_stats, it + 1)
                        pe.matmul(ps_o[:, 0:2 * CT], block_w[:], small[:, 0, :, :].rearrange("p k s -> p (k s)"),
                                  start=True, stop=True).then_inc(gn_means, 1)
                    elif kind == "qk":
                        _, st, g, w, hf = s
                        if st == 0:
                            pe.wait_ge(lo_ready, it * (CT + 2 * NH) + CT)
                        else:
                            pe.wait_ge(lo_ready, it * (CT + 2 * NH) + CT + (hf + 1 if g == 0 and w == "q" else NH))
                        acc = one(s)
                        m = 4 * st + "qk".index(w)
                        for k in range(CT):
                            mm = split(pe, acc, parts(m, k, P * g, P * g + P),
                                       acts(k, HALF * hf, HALF * hf + HALF), k == 0, k == CT - 1)
                        mm.then_inc(one_full[s_slot[s]], 1)
                    elif kind == "v":
                        _, st, n = s
                        acc = one(s)
                        for i in range(2):
                            at = (2 * n + i) * P
                            for k in range(CT):
                                mm = split(pe, acc[:, C * i:C * i + C], acts(k, at, at + P),
                                           parts(4 * st + 2, k, 0, C), k == 0, k == CT - 1)
                        mm.then_inc(one_full[s_slot[s]], 1)
                    elif kind == "top":
                        _, st, g, j, i = s
                        if j == 0 and i == 0:
                            pe.wait_ge(stacked[g], (it * 2 + st + 1) * 16 * n_stack_dma)
                        acc = two(s)
                        n_keys = cols(st, i)
                        for c0 in range(0, n_keys, HALF):
                            c1 = min(c0 + HALF, n_keys)
                            diag = st == 1 and c1 == n_keys
                            mm = pe.matmul(acc[:, c0:c1], q_st[0:MID, g, j, P * i:P * i + P],
                                           k_st[0:MID, g, j, c0:c1], start=True, stop=not diag)
                            if diag:
                                mm = pe.matmul(acc[:, c1 - P:c1], ident_bf[:], mask_qk[:], start=False, stop=True)
                        mm.then_inc(top_full[d_slot[s]], 1)
                    elif kind == "row":
                        _, st, g, j = s
                        pe.wait_ge(top_ready, it * n_row + row_no[s])
                        acc = two(s)
                        for i in range(TT):
                            mm = pe.matmul(acc[MID:MID + 1, P * i:P * i + P], tops[:, j, i:i + 1], minus_bf[:],
                                           start=True, stop=True)
                        mm.then_inc(top_full[d_slot[s]], 1)
                    elif kind == "mix":
                        _, st, g, hf, k = s
                        if hf == 0 and k == 0:
                            pe.wait_ge(row_ready, it * n_row + row_no[("row", st, g, G - 1)])
                        a = first(st, hf, k)
                        diag = st == 1 and k >= PH * hf
                        for j in range(G):
                            if j == 2 and k > 0:
                                multiply_values(("mix", st, g, hf, k - 1))
                            acc = one(s + (j,))
                            mm = pe.matmul(acc[:, a:HALF], k_st[0:MID + 1, g, j, P * k:P * k + P],
                                           q_st[0:MID + 1, g, j, HALF * hf + a:HALF * hf + HALF],
                                           start=True, stop=not diag)
                            if diag:
                                mm = pe.matmul(acc[:, a:a + P], ident_bf[:], mask_kq[:], start=False, stop=True)
                            mm.then_inc(one_full[s_slot[s + (j,)]], 1)
                    elif kind == "norm":
                        _, st, g, hf = s
                        multiply_values(("mix", st, g, hf, (PH * (hf + 1) if st else TT) - 1))
                    elif kind == "out":
                        _, st, hf, ct = s
                        pe.wait_ge(att_lo, it * n_norm + n_norm // 2 * st + n_norm // 2)
                        acc = one(s)
                        for k in range(CT):
                            mm = split(pe, acc, parts(4 * st + 3, k, P * ct, P * ct + P),
                                       acts(k, HALF * hf, HALF * hf + HALF), k == 0, k == CT - 1)
                        mm.then_inc(one_full[s_slot[s]], 1)
                    elif kind == "ln":
                        _, ln, hf = s
                        span = slice(HALF * hf, HALF * hf + HALF)
                        pe.wait_ge(x_res_ready, it * n_out + out_no[("out", ln, hf, CT - 1)])
                        acc = one(s + ("mean",))
                        for k in range(CT):
                            mm = pe.matmul(acc, mean_w[:], x_res[:, k, span], start=(k == 0), stop=(k == CT - 1))
                        mm.then_inc(one_full[s_slot[s + ("mean",)]], 1)
                        pe.wait_ge(squared, it * n_ln + ln_no[s])
                        acc = one(s + ("var",))
                        for k in range(CT):
                            mm = pe.matmul(acc, mean_w[:], probs[:, 0, k, :], start=(k == 0), stop=(k == CT - 1))
                        mm.then_inc(one_full[s_slot[s + ("var",)]], 1)
                    elif kind == "route":
                        pe.wait_ge(xn_ready, it * (CT + 2 * NH) + CT + 2 * NH)
                        for i in range(TT):
                            for k in range(CT):
                                mm = pe.matmul(ps_o[:, E * i:E * i + E], xn[:, k, P * i:P * i + P], sel_w[:, k, :],
                                               start=(k == 0), stop=(k == CT - 1))
                        mm.then_inc(logits, 1)
                        pe.wait_ge(gates, it + 1)
                        for hf in range(NH):
                            mm = pe.transpose(ps_s[:, P * hf:P * hf + P],
                                              w_tok[:, PH * hf:PH * hf + PH, :].rearrange("p i e -> p (i e)"),
                                              ident[:])
                        mm.then_inc(turned, 1)
                    elif kind in ("up", "down"):
                        n = MOE.index(s[1:]) if kind == "up" else n_up
                        if kind == "up":
                            _, j, hf = s
                            r = j % RING
                            pe.wait_ge(expert_in[r], (it * (ET // RING) + j // RING + 1) * 32)
                            acc = one(s)
                            for k in range(CT):
                                mm = pe.matmul(acc, keys_sb[:, r, k, :], xn[:, k, HALF * hf:HALF * hf + HALF],
                                               start=(k == 0), stop=(k == CT - 1))
                            mm.then_inc(one_full[s_slot[s]], 1)
                        if n:
                            j, hf = MOE[n - 1]
                            u = ("up", j, hf)
                            pe.wait_ge(one_free[s_slot[u]], it * s_uses[s_slot[u]] + s_use[u])
                            for ct in range(CT):
                                mm = pe.matmul(ps_top[:, hf, HALF * ct:HALF * ct + HALF],
                                               vals_sb[:, j % RING, P * ct:P * ct + P], gated[:, (n - 1) % 4, :],
                                               start=(j == 0), stop=(j == ET - 1))
                            mm.then_inc(downed, 1)

        @block.scalar
        def _(act):
            act.preload_act_table_set("natural_log_exp_and_others")
            staged = probs[:, :, :, :].rearrange("p a g t -> p (a g t)")
            act.wait_ge(weights_in, 64)
            act.copy(w_hi[:, :, :, :].rearrange("p m k c -> p (m k c)"), staged).then_inc(weights_hi, 1)
            with act.Fori(0, B) as it:
                for s in STEPS:
                    kind = s[0]

                    def full(u):
                        act.wait_ge(one_full[s_slot[u]], it * s_uses[s_slot[u]] + s_use[u])
                        return ps_one[:, s_slot[u], :]

                    def inverse_root(out_, var, n, ready):
                        act.activation(out_, var, ACT.Ln).then_inc(logged, 1)
                        act.wait_ge(logged, it * (1 + n_ln) + n)
                        act.activation(out_, out_, ACT.Exp, scale=-0.5).then_inc(ready, 1)

                    if kind == "gn":
                        act.wait_ge(gn_var, it + 1)
                        inverse_root(small[:, 5, :, 0], small[:, 4, :, 0], 1, gn_rstd)
                        for k in range(CT):
                            act.wait_ge(xn_ready, it * (CT + 2 * NH) + k + 1)
                            act.copy(act_hi[:, k, :], xn[:, k, :]).then_inc(hi_ready, 1)
                    elif kind == "qk":
                        _, st, g, w, hf = s
                        acc = full(s)
                        n = group_no[(st, g)] - 1
                        if n:
                            pst, pg = list(group_no)[n - 1]
                            act.wait_ge(stacked[pg], (it * 2 + pst + 1) * 16 * n_stack_dma)
                        m = 4 * st + "qk".index(w)
                        act.activation(nat_hi[:, "qk".index(w), HALF * hf:HALF * hf + HALF], acc, ACT.Identity,
                                       bias=bias[:, m, g:g + 1]).then_inc(nat_hi_ready, 1)
                    elif kind == "v":
                        _, st, n = s
                        acc = full(s)
                        act.copy(v_sb[:, 2 * n:2 * n + 2, :].rearrange("p i c -> p (i c)"),
                                 acc).then_inc(v_ready, 1)
                        act.wait_ge(v_ready, it * n_v + v_no[s])
                        act.sem_inc(one_free[s_slot[s]], 1)
                    elif kind == "row":
                        _, st, g, j = s
                        act.wait_ge(top_full[d_slot[s]], it * d_uses[d_slot[s]] + d_use[s])
                        act.copy(q_st[MID:MID + 1, g, j, :], ps_top[MID:MID + 1, d_slot[s], :]).then_inc(row_ready, 1)
                        act.wait_ge(row_ready, it * n_row + row_no[s])
                        act.sem_inc(top_free[d_slot[s]], 1)
                    elif kind == "mix":
                        _, st, g, hf, k = s
                        a = first(st, hf, k)
                        n = mix_no[s]
                        if n > 2:
                            act.wait_ge(mixed, it * n_mix + n - 2)
                        for j in range(G):
                            acc = full(s + (j,))
                            act.activation(probs[:, n % 2, j, a:HALF], acc[:, a:HALF], ACT.Exp,
                                           scale=SCALE).then_inc(one_free[s_slot[s + (j,)]], 1)
                    elif kind == "norm":
                        _, st, g, hf = s
                        act.wait_ge(norm_done, it * n_norm + norm_no[s])
                        act.activation(act_hi[:, g, HALF * hf:HALF * hf + HALF], rsum[:], ACT.Identity,
                                       bias=bias[:, 4 * st + 2, g:g + 1]).then_inc(att_hi, 1)
                    elif kind == "ln":
                        _, ln, hf = s
                        span = slice(HALF * hf, HALF * hf + HALF)
                        act.wait_ge(centred, it * n_ln + ln_no[s])
                        if hf:
                            act.wait_ge(var_ready, it * n_ln + ln_no[s] - 1)
                        act.activation(probs[:, 0, 0:CT, :], xn[:, :, span], ACT.Square).then_inc(squared, 1)
                        act.wait_ge(var_ready, it * n_ln + ln_no[s])
                        inverse_root(rstd[:], var_sb[:], 1 + ln_no[s], rstd_ready)
                        act.wait_ge(xn_ready, it * (CT + 2 * NH) + CT + ln_no[s])
                        act.copy(act_hi[:, :, span], xn[:, :, span]).then_inc(hi_ready, 1)
                    elif kind == "route":
                        act.wait_ge(logits, it + 1)
                        act.activation(w_tok[:, :, :], ps_o[:, 0:TT * E].rearrange("p (i e) -> p i e", e=E),
                                       ACT.Exp, scale=-1.0).then_inc(sel_exp, 1)

        @block.vector
        def _(dve):
            staged = probs[:, :, :, :].rearrange("p a g t -> p (a g t)")
            dve.sem_inc(batch_over, 1)
            dve.sem_inc(store_over, 1)
            dve.memset(f(k_st[MID:MID + 1, :, :, :]), 1.0).then_inc(fills, 1)
            dve.memset(pad_sel[:], -1.0).then_inc(fills, 1)
            dve.wait_ge(weights_hi, 1)
            dve.wait_ge(weights_in, 64)
            dve.tensor_tensor(w_lo[:, :, :, :].rearrange("p m k c -> p (m k c)"), staged,
                              f(w_hi[:, :, :, :].rearrange("p m k c -> p (m k c)")),
                              ALU.subtract).then_inc(weights_lo, 1)
            dve.wait_ge(consts, N_CONSTS)
            dve.wait_ge(weights_lo, 1)
            dve.wait_ge(fills, 2)
            links = VEC_LINKS
            with dve.Fori(0, B) as it:
                count = [0]

                def link(ins):
                    count[0] += 1
                    ins.then_inc(vec, 1)
                    dve.wait_ge(vec, it * links + count[0])

                def full(u):
                    dve.wait_ge(one_full[s_slot[u]], it * s_uses[s_slot[u]] + s_use[u])
                    return ps_one[:, s_slot[u], :]

                def refine(y, var, tmp):
                    link(dve.tensor_tensor(tmp, var, y, ALU.mult))
                    link(dve.tensor_tensor(tmp, tmp, y, ALU.mult))
                    link(dve.tensor_scalar(tmp, tmp, -0.5, 1.5, ALU.mult, ALU.add))
                    link(dve.tensor_tensor(y, y, tmp, ALU.mult))

                for s in STEPS:
                    kind = s[0]
                    if kind == "gn":
                        dve.wait_ge(x_loaded, (it + 1) * 16)
                        dve.wait_ge(store_over, it + 1)
                        for k in range(CT):
                            for hf in range(NH):
                                ins = dve.bn_stats(st6[:, k, hf, :], x_in[:, k, HALF * hf:HALF * hf + HALF])
                        link(ins)
                        dve.sem_inc(passed, 1)
                        for k in range(CT):
                            ins = dve.bn_aggr(mv[:, k, :], st6[:, k, :, :].rearrange("p h s -> p (h s)"))
                        link(ins)
                        link(dve.tensor_copy(small[:, 0, :, 0], mv[:, :, 0]))
                        link(dve.tensor_tensor(small[:, 1, :, 0], mv[:, :, 0], mv[:, :, 0], ALU.mult))
                        dve.tensor_tensor(small[:, 0, :, 1], small[:, 1, :, 0], mv[:, :, 1],
                                          ALU.add).then_inc(gn_stats, 1)
                        dve.wait_ge(gn_means, it + 1)
                        link(dve.tensor_copy(small[:, 2, :, :].rearrange("p k s -> p (k s)"), ps_o[:, 0:2 * CT]))
                        link(dve.tensor_tensor(small[:, 3, :, 0], small[:, 2, :, 0], small[:, 2, :, 0], ALU.mult))
                        link(dve.tensor_tensor(small[:, 3, :, 1], small[:, 2, :, 1], small[:, 3, :, 0],
                                               ALU.subtract))
                        dve.tensor_scalar(small[:, 4, :, 0], small[:, 3, :, 1], 1e-5, None,
                                          ALU.add).then_inc(gn_var, 1)
                        dve.wait_ge(gn_rstd, it + 1)
                        refine(small[:, 5, :, 0], small[:, 4, :, 0], small[:, 5, :, 1])
                        link(dve.tensor_tensor(small[:, 6, :, 0], small[:, 5, :, 0], gnw[:, 0, :], ALU.mult))
                        link(dve.tensor_tensor(small[:, 6, :, 1], small[:, 2, :, 0], small[:, 6, :, 0], ALU.mult))
                        link(dve.tensor_tensor(small[:, 7, :, 0], gnw[:, 1, :], small[:, 6, :, 1], ALU.subtract))
                        for k in range(CT):
                            dve.tensor_scalar(xn[:, k, :], x_in[:, k, :], small[:, 6, k, 0:1],
                                              small[:, 7, k, 0:1], ALU.mult, ALU.add).then_inc(xn_ready, 1)
                        for k in range(CT):
                            dve.wait_ge(hi_ready, it * (CT + 2 * NH) + k + 1)
                            dve.wait_ge(xn_ready, it * (CT + 2 * NH) + k + 1)
                            dve.tensor_tensor(act_lo[:, k, :], xn[:, k, :], f(act_hi[:, k, :]),
                                              ALU.subtract).then_inc(lo_ready, 1)
                    elif kind == "qk":
                        _, st, g, w, hf = s
                        m, n = 4 * st + "qk".index(w), "qk".index(w)
                        acc = full(s)
                        dve.wait_ge(nat_hi_ready, it * n_qk + qk_no[s])
                        span = slice(HALF * hf, HALF * hf + HALF)
                        dve.scalar_tensor_tensor(out=nat_lo[:, n, span], in0=acc, scalar=bias[:, m, g:g + 1],
                                                 in1=f(nat_hi[:, n, span]), op0=ALU.add,
                                                 op1=ALU.subtract).then_inc(nat_lo_ready, 1)
                        dve.wait_ge(nat_lo_ready, it * n_qk + qk_no[s])
                        dve.sem_inc(one_free[s_slot[s]], 1)
                    elif kind == "top":
                        _, st, g, j, i = s
                        dve.wait_ge(top_full[d_slot[s]], it * d_uses[d_slot[s]] + d_use[s])
                        if i == 0 and row_no[("row", st, g, j)] > G:
                            dve.wait_ge(row_ready, it * n_row + row_no[("row", st, g, j)] - G)
                        dve.reduce_max(tops[:, j, i:i + 1], ps_top[:, d_slot[s], 0:cols(st, i)],
                                       AX_X).then_inc(top_free[d_slot[s]], 1)
                    elif kind == "row":
                        for slot in range(2):
                            last = max(d_use[u] for u in double
                                       if d_slot[u] == slot and double.index(u) < double.index(s))
                            dve.wait_ge(top_free[slot], it * d_uses[slot] + last)
                        dve.sem_inc(top_ready, 1)
                    elif kind == "norm":
                        _, st, g, hf = s
                        k = (PH * (hf + 1) if st else TT) - 1
                        dve.wait_ge(mixed, it * n_mix + mix_no[("mix", st, g, hf, k)])
                        if norm_no[s] > 1:
                            dve.wait_ge(att_lo, it * n_norm + norm_no[s] - 1)
                        link(dve.reciprocal(rsum[:], ps_s[:]))
                        dve.tensor_tensor(rsum[:], ps_o[:], rsum[:], ALU.mult).then_inc(norm_done, 1)
                        dve.wait_ge(norm_done, it * n_norm + norm_no[s])
                        dve.wait_ge(att_hi, it * n_norm + norm_no[s])
                        span = slice(HALF * hf, HALF * hf + HALF)
                        dve.scalar_tensor_tensor(out=act_lo[:, g, span], in0=rsum[:],
                                                 scalar=bias[:, 4 * st + 2, g:g + 1], in1=f(act_hi[:, g, span]),
                                                 op0=ALU.add, op1=ALU.subtract).then_inc(att_lo, 1)
                    elif kind == "out":
                        _, st, hf, ct = s
                        span = slice(HALF * hf, HALF * hf + HALF)
                        acc = full(s)
                        before = x_res if st else x_in
                        dve.scalar_tensor_tensor(out=x_res[:, ct, span], in0=acc, scalar=bias[:, 4 * st + 3, ct:ct + 1],
                                                 in1=before[:, ct, span], op0=ALU.add,
                                                 op1=ALU.add).then_inc(x_res_ready, 1)
                        dve.wait_ge(x_res_ready, it * n_out + out_no[s])
                        dve.sem_inc(one_free[s_slot[s]], 1)
                    elif kind == "ln":
                        _, ln, hf = s
                        span = slice(HALF * hf, HALF * hf + HALF)
                        acc = full(s + ("mean",))
                        for k in range(CT):
                            link(dve.tensor_tensor(xn[:, k, span], x_res[:, k, span], acc, ALU.subtract))
                        dve.sem_inc(centred, 1)
                        dve.sem_inc(one_free[s_slot[s + ("mean",)]], 1)
                        acc = full(s + ("var",))
                        dve.tensor_scalar(var_sb[:], acc, 1e-5, None, ALU.add).then_inc(var_ready, 1)
                        dve.wait_ge(var_ready, it * n_ln + ln_no[s])
                        dve.sem_inc(one_free[s_slot[s + ("var",)]], 1)
                        dve.wait_ge(rstd_ready, it * n_ln + ln_no[s])
                        refine(rstd[:], var_sb[:], rsum[:])
                        for k in range(CT):
                            link(dve.tensor_tensor(xn[:, k, span], xn[:, k, span], rstd[:], ALU.mult))
                        dve.sem_inc(xn_ready, 1)
                        dve.wait_ge(hi_ready, it * (CT + 2 * NH) + CT + ln_no[s])
                        dve.tensor_tensor(act_lo[:, :, span], xn[:, :, span], f(act_hi[:, :, span]),
                                          ALU.subtract).then_inc(lo_ready, 1)
                    elif kind == "route":
                        dve.wait_ge(sel_exp, it + 1)
                        link(dve.tensor_scalar(w_tok[:], w_tok[:], 1.0, None, ALU.add))
                        link(dve.reciprocal(pad_sel[:, :, 0:E], w_tok[:]))
                        dve.sem_inc(passed, 1)
                        for i in range(TT):
                            ins = dve.max(top8[:, i, :], pad_sel[:, i, 0:E])
                        link(ins)
                        link(dve.memset(top8[:, :, 2:8], -1.0))
                        dve.sem_inc(passed, 1)
                        for i in range(TT):
                            ins = dve.match_replace(rest[:, i, :], top8[:, i, :], pad_sel[:, i, :], 0.0)
                        link(ins)
                        dve.tensor_tensor(w_tok[:], pad_sel[:, :, 0:E], rest[:, :, 0:E],
                                          ALU.subtract).then_inc(gates, 1)
                        dve.wait_ge(turned, it + 1)
                        dve.tensor_copy(w_turn[:].rearrange("p h t -> p (h t)"),
                                        ps_s[:, 0:NH * P]).then_inc(turned_sb, 1)
                    elif kind == "up":
                        _, j, hf = s
                        n = MOE.index((j, hf))
                        acc = full(s)
                        dve.wait_ge(gate_in[j % 2], (it * (ET // 2) + j // 2 + 1) * 16 * EPT)
                        if n >= 4:
                            dve.wait_ge(downed, it * n_up + n - 3)
                        dve.scalar_tensor_tensor(out=gated[:, n % 4, :], in0=acc, scalar=0.0,
                                                 in1=gate_bc[:, j % 2, HALF * hf:HALF * hf + HALF],
                                                 op0=ALU.max, op1=ALU.mult).then_inc(one_free[s_slot[s]], 1)
                    elif kind == "down":
                        dve.wait_ge(downed, (it + 1) * n_up)
                        for hf in range(NH):
                            for ct in range(CT):
                                dve.tensor_tensor(x_res[:, ct, HALF * hf:HALF * hf + HALF],
                                                  ps_top[:, hf, HALF * ct:HALF * ct + HALF],
                                                  x_res[:, ct, HALF * hf:HALF * hf + HALF],
                                                  ALU.add).then_inc(result, 1)
                        dve.wait_ge(result, (it + 1) * NH * CT)
                        dve.sem_inc(batch_over, 1)
                assert count[0] == links, count[0]


VEC_LINKS = 59
N_CONSTS = 15


def nc_next(sp, it, batches):
    return (it + 1) % batches


def kernel(**inputs):
    import concourse.bacc as bacc
    from concourse.bass_utils import run_bass_kernel_spmd

    a = {n: np.asarray(v) for n, v in inputs.items()}
    B, C, Hh, Ww = a["x"].shape
    T = Hh * Ww
    CT = C // P
    heads = 8
    ch = C // heads
    qkv = a["L0_conv_qkv_w"].reshape(heads, 3, ch, C)
    qkv_b = a["L0_conv_qkv_b"].reshape(heads, 3, ch)
    mats = [qkv[:, n].reshape(C, C).T for n in range(3)] + [a["L0_conv_proj_w"].T]
    mats += [a["L1_attn_W_" + n] for n in "QKVO"]
    vecs = [qkv_b[:, n].reshape(C) for n in range(3)] + [a["L0_conv_proj_b"]]
    vecs += [a["L1_attn_b_" + n] for n in "QKVO"]
    keys = a["L1_ffn_keys"]
    E, _, H = keys.shape
    ET = E * H // P

    def by_partition(m):
        return np.moveaxis(m.reshape(m.shape[:-1] + (CT, P)), -1, 0)

    arrays = {
        "x_in_dram": a["x"].reshape(B, C, T),
        "mats_dram": np.stack(mats).reshape(8, CT, P, C).transpose(2, 0, 1, 3),
        "vecs_dram": by_partition(np.stack(vecs)),
        "norm_dram": by_partition(np.stack([a["L0_conv_norm_w"], a["L0_conv_norm_b"]])),
        "sel_dram": a["L1_ffn_expert_sel"].T.reshape(CT, P, E).transpose(1, 0, 2),
        "keys_dram": keys.transpose(1, 0, 2).reshape(CT, P, ET, P).transpose(1, 2, 0, 3),
        "values_dram": a["L1_ffn_values"].reshape(E * H, C),
    }
    arrays = {n: np.ascontiguousarray(v) for n, v in arrays.items()}
    nc = bacc.Bacc("TRN2", target_bir_lowering=False, num_devices=1)
    args = [nc.dram_tensor(n, v.shape, mybir.dt.from_np(v.dtype), kind="ExternalInput").ap()
            for n, v in arrays.items()]
    out = nc.dram_tensor("out_dram", (B, C, T), F32, kind="ExternalOutput").ap()
    w_dram = nc.dram_tensor("gates_dram", (E, T), F32, kind="Internal").ap()
    bass_hybrid_kernel(nc, *args, out, w_dram)
    r = run_bass_kernel_spmd(nc, [arrays], core_ids=[0])
    return r.results[0]["out_dram"].reshape(B, C, Hh, Ww)
```

```python
from contextlib import ExitStack

import numpy as np

import concourse.bass as bass
from concourse import mybir

ACT = mybir.ActivationFunctionType
ALU = mybir.AluOpType
AX_X = mybir.AxisListType.X
F32 = mybir.dt.float32
F32R = mybir.dt.float32r
BF16 = mybir.dt.bfloat16

P = 128
HALF = 512
HEADS_PER_GROUP = 4
MASKED = -1.0e30


def spread(main, side):
    out, done = [], 0
    for n, step in enumerate(main):
        out.append(step)
        upto = len(side) * (n + 1) // len(main)
        out += side[done:upto]
        done = upto
    return out


class Steps:

    def __init__(self, tiles, halves, channel_tiles, expert_tiles):
        self.tiles, self.halves, self.groups, self.experts = tiles, halves, channel_tiles, expert_tiles

    def qk(self, st, g, halves=None):
        out = []
        for hf in range(self.halves) if halves is None else halves:
            out += [("qk", st, g, "q", hf), ("qk", st, g, "k", hf), ("stack", st, g, hf)]
        return out

    def v(self, st):
        return [("v", st, n) for n in range(self.tiles // 2)]

    def top(self, st, g, hf):
        per_half = self.tiles // self.halves
        out = []
        for j in range(HEADS_PER_GROUP):
            out += [("top", st, g, j, i) for i in range(per_half * hf, per_half * (hf + 1))] + [("row", st, g, j, hf)]
        return out

    def mix(self, st, g, hf, wide, late=()):
        last = self.tiles // self.halves * (hf + 1) if st else self.tiles
        steps = [("mix", st, g, hf, k, wide) for k in range(last)]
        return steps[:2] + list(late) + steps[2:] + [("norm", st, g, hf)]

    def out(self, st, hf):
        return [("out", st, hf, ct) for ct in range(self.groups)]

    def first(self):
        return [("gn",), ("split", 0), ("split", 1)] + self.qk(0, 0) + self.v(0)[:2]

    def experts_of(self, tops):
        ups = [("up", hf, j) for hf in range(self.halves) for j in range(self.experts)]
        steps = spread(ups, tops) if tops else ups
        at = steps.index(("up", 0, self.experts - 1)) + 1
        return steps[:at] + [("down", 0)] + steps[at:] + [("down", 1)]

    def batch(self, experts):
        tops = self.top(0, 0, 0) + self.top(0, 0, 1) + self.top(0, 1, 0) + self.top(0, 1, 1)
        steps = self.v(0)[2:] + self.qk(0, 1)
        if experts:
            steps += tops[:10] + [("turn",)] + tops[10:14] + self.experts_of(tops[14:])
        else:
            steps += tops
        steps += self.mix(0, 0, 0, True)
        steps += self.mix(0, 0, 1, True, [("fin", 0, 0, 0)])
        steps += self.mix(0, 1, 0, True, [("fin", 0, 0, 1)])
        main = self.mix(0, 1, 1, True, [("fin", 0, 1, 0)] + self.out(0, 0))[:-1]
        side = [("lna", 0, 0), ("lnb", 0, 0)] + self.qk(1, 0, [0]) + self.top(1, 0, 0)
        side = side[:15] + self.v(1)[:2] + side[15:]
        steps += main[:5] + spread(main[5:], side) + [("norm", 0, 1, 1)]
        steps += self.qk(1, 1, [0]) + [("fin", 0, 1, 1)] + self.out(0, 1) + [("lna", 0, 1)]
        main = self.mix(1, 0, 0, False)
        steps += spread(main[:2], self.top(1, 1, 0)) + [("lnb", 0, 1)] + main[2:]
        steps += self.qk(1, 0, [1]) + [("fin", 1, 0, 0)] + self.v(1)[2:] + self.qk(1, 1, [1])
        steps += spread(self.mix(1, 1, 0, False), self.top(1, 0, 1))
        steps += spread(self.mix(1, 0, 1, False, [("fin", 1, 1, 0)]), self.top(1, 1, 1))
        main = self.mix(1, 1, 1, True, [("fin", 1, 0, 1), ("gn",)] + self.out(1, 0))[:-1]
        side = [("lna", 1, 0), ("lnb", 1, 0), ("split", 0)] + self.qk(0, 0, [0])
        steps += main[:5] + spread(main[5:], side) + [("norm", 1, 1, 1), ("fin", 1, 1, 1)] + self.out(1, 1)
        v, ahead = self.v(0)[:2], self.qk(0, 0, [1])
        steps += [("lna", 1, 1), v[0], ("split", 1), ("lnb", 1, 1), v[1]] + ahead + [("logits",)]
        return steps

    def last(self):
        return [("turn",)] + self.experts_of([])


LINKS = {"gn": 11, "norm": 1, "lna": 1, "lnb": 5, "logits": 5}
N_CONSTS = 15


def events(steps):
    kinds = {}

    def add(kind, key):
        kinds.setdefault(kind, {})[key] = len(kinds.get(kind, {})) + 1

    turn = {"one": 0, "two": 0}

    def use(bank, key):
        add(f"{bank}{turn[bank] % 2}", key)
        turn[bank] += 1

    for s in steps:
        kind = s[0]
        add(kind, s)
        if kind in ("gn", "qk", "v", "out", "lna", "lnb", "logits", "turn", "up"):
            use("one", s)
        if kind == "mix":
            for n in range(2 if s[5] else HEADS_PER_GROUP):
                use("two" if s[5] else "one", s + (n,))
        if kind in ("top", "row"):
            use("two", s)
        if kind in ("norm", "down"):
            add("acc", s)
        if kind == "split" or kind == "lnb" and s[1] == 0:
            add("acts", s)
        if kind == "stack":
            add(f"stacks{s[2]}{s[3]}", s[:3])
        for n in range(LINKS.get(kind, 0)):
            add("link", s + (n,))
    return kinds


def bass_hybrid_kernel(nc: bass.Bass, x, mats, vecs, norm_wb, sel_t, experts, out, w_dram):
    B, C, T = x.shape
    E = sel_t.shape[2]
    H = experts.shape[0] * P // E
    CT = C // P
    NH = T // HALF
    TT = T // P
    PH = HALF // P
    G = HEADS_PER_GROUP
    HD = P // G
    MID = 3 * HD
    ET = E * H // P
    EPT = P // H
    RING = 4
    SCALE = float(HD) ** -0.5
    NORM_GROUP = C // 32
    STACK = 16 * 3
    assert NH == 2 and ET * NH % RING == 0

    plan = Steps(TT, NH, CT, ET)
    SECTIONS = {"first": plan.first(), "head": plan.batch(False), "body": plan.batch(True), "last": plan.last()}
    EVENTS = {name: events(steps) for name, steps in SECTIONS.items()}

    BEFORE = {"first": [], "head": ["first"], "body": ["first", "head"], "last": ["first", "head"]}

    class Section:

        def __init__(self, name, it=None):
            self.name, self.it = name, it
            self.steps, self.no = SECTIONS[name], EVENTS[name]

        def total(self, name, kind):
            return len(EVENTS[name].get(kind, {}))

        def value(self, kind, n, each=1):
            n += sum(self.total(b, kind) for b in BEFORE[self.name])
            if self.name == "body":
                return ((self.it - 1) * self.total("body", kind) + n) * each
            if self.name == "last":
                return ((B - 1) * self.total("body", kind) + n) * each
            return n * each

        def any(self, kind, n):
            value = n + sum(self.total(b, kind) for b in BEFORE[self.name])
            return value + ((B - 1) * self.total("body", kind) if self.name == "last" else 0) > 0

        def bank(self, u):
            return next((b, self.no[b][u]) for b in ("one0", "one1", "two0", "two1") if u in self.no.get(b, {}))

    def cols(st, i):
        return P * (i + 1) if st else T

    def first(st, hf, k):
        return max(0, P * (k - PH * hf)) if st else 0

    def last_tile(st, hf):
        return (PH * (hf + 1) if st else TT) - 1

    def last_mix(sec, s):
        _, st, g, hf = s
        return next(m for m in sec.no["mix"] if m[1:5] == (st, g, hf, last_tile(st, hf)))

    def half(hf):
        return slice(HALF * hf, HALF * hf + HALF)

    with ExitStack() as ctx:
        def sb(name, shape, dt=F32):
            return ctx.enter_context(nc.sbuf_tensor(name, shape, dt))

        def sem(name):
            return ctx.enter_context(nc.semaphore(name))

        w_hi = sb("w_hi", [P, 8, CT, C], F32R)
        w_lo = sb("w_lo", [P, 8, CT, C], F32R)
        bias = sb("bias", [P, 8, CT])
        gnw = sb("gnw", [P, 2, CT])
        sel_w = sb("sel_w", [P, CT, E])
        ident = sb("ident", [P, P])
        ident_bf = sb("ident_bf", [P, P], BF16)
        minus_bf = sb("minus_bf", [P, P], BF16)
        mask_qk = sb("mask_qk", [P, P], BF16)
        mask_kq = sb("mask_kq", [P, P], BF16)
        mean_w = sb("mean_w", [P, P])
        block_w = sb("block_w", [P, P])
        ones32 = sb("ones32", [P, HD])

        x_in = sb("x_in", [P, CT, T])
        x_res = sb("x_res", [P, CT, T])
        xt = sb("xt", [P, CT, HALF])
        xn = sb("xn", [P, CT, T])
        act_hi = sb("act_hi", [P, CT, T], F32R)
        act_lo = sb("act_lo", [P, CT, T], F32R)
        nat = sb("nat", [P, 4, T], F32R)
        stacks = sb("stacks", [P, 2, CT, G, T], F32R)
        q_st, k_st = stacks[:, 0, :, :, :], stacks[:, 1, :, :, :]
        v_sb = sb("v_sb", [P, TT, C])
        probs = sb("probs", [P, 2, G, HALF])
        squares = sb("squares", [P, CT, HALF])
        tops = sb("tops", [P, G, TT], BF16)
        rsum = sb("rsum", [P, HALF])
        o_sb = sb("o_sb", [P, HALF])
        var_sb = sb("var_sb", [P, HALF])
        rstd = sb("rstd", [P, HALF])
        st6 = sb("st6", [P, CT, NH, 6])
        mv = sb("mv", [P, CT, 2])
        small = sb("small", [P, 8, CT, 2])
        expert_sb = sb("expert_sb", [P, RING, CT * P + C])
        keys_sb = expert_sb[:, :, 0:CT * P].rearrange("p r (k c) -> p r k c", k=CT)
        vals_sb = expert_sb[:, :, CT * P:CT * P + C]
        pad_sel = sb("pad_sel", [P, TT, E + 8])
        top8 = sb("top8", [P, TT, 8])
        w_turn = sb("w_turn", [P, NH, P])
        rtmp = squares[:, 0, :]
        w_tok = squares[:, 0, 0:TT * E].rearrange("p (i e) -> p i e", e=E)
        rest = squares[:, 1, 0:TT * (E + 8)].rearrange("p (i e) -> p i e", e=E + 8)
        gated = probs[:, 0, :, :]
        gate_bc = probs[:, 1, :, :]

        ps_two = ctx.enter_context(nc.psum_tensor("ps_two", [P, 2, T], F32))
        ps_one = ctx.enter_context(nc.psum_tensor("ps_one", [P, 2, HALF], F32))
        ps_acc = ctx.enter_context(nc.psum_tensor("ps_acc", [P, 2, HALF], F32))

        passed = sem("passed")
        passed_too = sem("passed_too")
        consts = sem("consts")
        fills = sem("fills")
        weights_in = sem("weights_in")
        weights_hi = sem("weights_hi")
        weights_lo = sem("weights_lo")
        x_loaded = sem("x_loaded")
        bank_full = {b: sem(f"{b}_full") for b in ("one0", "one1", "two0", "two1")}
        bank_read = {b: sem(f"{b}_read") for b in ("one0", "one1", "two0", "two1")}
        squared_read = sem("squared_read")
        offsets = sem("offsets")
        linked = sem("linked")
        gn_stats = sem("gn_stats")
        gn_var = sem("gn_var")
        gn_root = sem("gn_root")
        xt_ready = sem("xt_ready")
        logged = sem("logged")
        ln_root = sem("ln_root")
        xn_ready = sem("xn_ready")
        acts_hi = sem("acts_hi")
        acts_lo = sem("acts_lo")
        nat_hi_ready = sem("nat_hi_ready")
        stacked = [[[sem(f"stacked{g}_{hf}_{j}") for j in range(G)] for hf in range(NH)] for g in range(CT)]
        v_ready = sem("v_ready")
        row_ready = sem("row_ready")
        mixed = sem("mixed")
        acc_read = sem("acc_read")
        out_read = sem("out_read")
        att_ready = sem("att_ready")
        att_hi = sem("att_hi")
        att_lo = sem("att_lo")
        squared = sem("squared")
        gates = sem("gates")
        gates_out = sem("gates_out")
        gate_in = [sem(f"gate_in{n}") for n in range(RING)]
        expert_in = [sem(f"expert_in{n}") for n in range(RING)]
        downed = sem("downed")
        stored = [sem(f"stored{hf}") for hf in range(NH)]

        def f(ap):
            return ap.bitcast(F32)

        def run(eng, emit):
            emit(Section("first"), None)
            emit(Section("head"), 0)
            with eng.Fori(1, B) as it:
                emit(Section("body", it), it)
            emit(Section("last"), B)

        block = ctx.enter_context(nc.Block())

        @block.sync
        def _(sp):
            sp.dma_start(x_in[:, :, :], x[0].rearrange("(k p) t -> p k t", p=P)).then_inc(x_loaded, 16)
            sp.dma_start(probs[:, :, :, :].rearrange("p a g t -> p (a g t)"),
                         mats.rearrange("p m k c -> p (m k c)")).then_inc(weights_in, 16)
            sp.dma_start(bias[:, :, :], vecs).then_inc(weights_in, 16)
            sp.dma_start(gnw[:, :, :], norm_wb).then_inc(weights_in, 16)
            sp.dma_start(sel_w[:, :, :], sel_t).then_inc(weights_in, 16)

            def emit(sec, it):
                def hold(semaphore, kind, n, each=1):
                    sp.wait_ge(semaphore, sec.value(kind, n, each))
                    sp.sem_inc(passed, 1)

                def read(u):
                    b, n = sec.bank(u)
                    hold(bank_read[b], b, n)

                for s in sec.steps:
                    if s[0] == "stack":
                        _, st, g, hf = s
                        read(("qk", st, g, "q", hf))
                        read(("qk", st, g, "k", hf))
                        if st:
                            hold(acc_read, "acc", sec.no["acc"][("norm", 0, g, NH - 1)])
                        elif g == 0 and sec.name != "first":
                            hold(acc_read, "acc", sec.no["acc"][("norm", 1, g, NH - 1)])
                        elif sec.name == "body":
                            hold(acc_read, "acc", 0)
                        for j in range(G):
                            rows = slice(HD * j, HD * j + HD)
                            for quad, pair in enumerate((slice(0, 4, 2), slice(0, 4, 3), slice(1, 3, 1))):
                                sp.dma_start(f(stacks[HD * quad:HD * quad + HD, :, g, j, half(hf)]),
                                             f(nat[rows, pair, half(hf)])).then_inc(stacked[g][hf][j], 16)
                    if s == ("out", 0, NH - 1, CT - 1):
                        read(s)
                        sp.dma_start(x_in[:, :, :],
                                     x[bass.ds(next_batch(it, B), 1)].rearrange("a (k p) t -> p (a k) t", p=P)
                                     ).then_inc(x_loaded, 16)
                    if s[0] == "turn":
                        read(s)
                        for i in range(TT):
                            sp.dma_start(w_dram[:, P * i:P * i + P],
                                         w_turn[E * (i % PH):E * (i % PH) + E, i // PH, :]).then_inc(gates_out, 16)
                    if s[0] == "down":
                        hf = s[1]
                        hold(acc_read, "acc", sec.no["acc"][s])
                        where = out[B - 1:B] if sec.name == "last" else out[bass.ds(it - 1, 1)]
                        sp.dma_start(where.rearrange("a (k p) t -> p (a k) t", p=P)[:, :, half(hf)],
                                     x_res[:, :, half(hf)]).then_inc(stored[hf], 16)

            run(sp, emit)
            last = Section("last")
            sp.wait_ge(gates_out, last.value("turn", 1, 16 * TT))
            for hf in range(NH):
                sp.wait_ge(stored[hf], last.value("turn", 1, 16))

        @block.gpsimd
        def _(pool):
            pool.memset(ident[:], 0.0).then_inc(consts, 1)
            pool.memset(ident_bf[:], 0.0).then_inc(consts, 1)
            pool.memset(minus_bf[:], 0.0).then_inc(consts, 1)
            pool.memset(mask_qk[:], 0.0).then_inc(consts, 1)
            pool.memset(mask_kq[:], 0.0).then_inc(consts, 1)
            pool.memset(block_w[:], 1.0 / NORM_GROUP).then_inc(consts, 1)
            pool.memset(mean_w[:], 1.0 / C).then_inc(consts, 1)
            pool.memset(ones32[:], 1.0).then_inc(consts, 1)
            pool.wait_ge(consts, 8)
            for m, value in ((ident, 1.0), (ident_bf, 1.0), (minus_bf, -1.0)):
                pool.affine_select(out=m[:], in_=m[:], compare_op=ALU.not_equal, fill=value, base=0,
                                   pattern=[[-1, P]], channel_multiplier=1).then_inc(consts, 1)
            pool.affine_select(out=mask_qk[:], in_=mask_qk[:], compare_op=ALU.is_ge, fill=MASKED, base=0,
                               pattern=[[-1, P]], channel_multiplier=1).then_inc(consts, 1)
            pool.affine_select(out=mask_kq[:], in_=mask_kq[:], compare_op=ALU.is_ge, fill=MASKED, base=0,
                               pattern=[[1, P]], channel_multiplier=-1).then_inc(consts, 1)
            blocks = block_w[:].rearrange("p (n e) -> p n e", e=NORM_GROUP)
            pool.affine_select(out=blocks, in_=blocks, compare_op=ALU.is_ge, fill=0.0, base=0,
                               pattern=[[-NORM_GROUP, P // NORM_GROUP], [0, NORM_GROUP]],
                               channel_multiplier=1).then_inc(consts, 1)
            pool.wait_ge(consts, 14)
            pool.affine_select(out=blocks, in_=blocks, compare_op=ALU.is_ge, fill=0.0, base=NORM_GROUP - 1,
                               pattern=[[NORM_GROUP, P // NORM_GROUP], [0, NORM_GROUP]],
                               channel_multiplier=-1).then_inc(consts, 1)

            def emit(sec, it):
                def hold(semaphore, kind, n, each=1):
                    pool.wait_ge(semaphore, sec.value(kind, n, each))
                    pool.sem_inc(passed_too, 1)

                def load_expert(m):
                    pool.dma_start(expert_sb[:, m % RING, :], experts[m % ET]).then_inc(expert_in[m % RING], 16)

                def load_gates(m):
                    hf, j = divmod(m, ET)
                    row = w_dram[EPT * j:EPT * j + EPT, half(hf)]
                    pool.dma_start(gate_bc[:, m % RING, :],
                                   bass.AP(row.tensor, row.offset, [[T, EPT], [0, H], [1, HALF]])
                                   ).then_inc(gate_in[m % RING], 16)

                for s in sec.steps:
                    if s[0] == "turn":
                        hold(acc_read, "acc", 0)
                        for m in range(RING):
                            load_expert(m)
                        hold(gates_out, "turn", sec.no["turn"][s], 16 * TT)
                        for m in range(RING):
                            load_gates(m)
                    if s[0] == "up":
                        m = s[1] * ET + s[2]
                        if 1 <= m and m - 1 + RING < NH * ET:
                            hold(downed, "up", m)
                            load_expert(m - 1 + RING)
                            load_gates(m - 1 + RING)

            run(pool, emit)

        @block.tensor
        def _(pe):
            def split(acc, lhs, rhs, start, stop):
                (lh, ll), (rh, rl) = lhs, rhs
                pe.matmul(acc, lh, rh, start=start, stop=False)
                pe.matmul(acc, lh, rl, start=False, stop=False)
                return pe.matmul(acc, ll, rh, start=False, stop=stop)

            def parts(m, k, lo, hi):
                return w_hi[:, m, k, lo:hi], w_lo[:, m, k, lo:hi]

            def acts(k, lo, hi):
                return act_hi[:, k, lo:hi], act_lo[:, k, lo:hi]

            def emit(sec, it):
                def bank(u):
                    b, n = sec.bank(u)
                    if sec.any(b, n - 1):
                        pe.wait_ge(bank_read[b], sec.value(b, n - 1))
                    return (ps_one if b[:3] == "one" else ps_two)[:, int(b[3]), :]

                def filled(mm, u):
                    mm.then_inc(bank_full[sec.bank(u)[0]], 1)

                def read(u):
                    b, n = sec.bank(u)
                    pe.wait_ge(bank_read[b], sec.value(b, n))

                def maxima(s):
                    _, st, g, j, hf = s
                    u = ("top", st, g, j, PH * hf + PH - 1)
                    others = [("top", st, g, j, i) for i in range(PH * hf, PH * hf + PH - 1)]
                    others = [o for o in others if sec.bank(o)[0] != sec.bank(u)[0]]
                    return others[-1:] + [u]

                def times_values(s):
                    _, st, g, hf, k, wide = s
                    a = first(st, hf, k)
                    n = 2 if wide else G
                    read(s + (n - 2,))
                    read(s + (n - 1,))
                    if k == 0:
                        if g == 0:
                            pe.wait_ge(v_ready, sec.value("v", sec.no["v"][("v", st, (last_tile(st, hf) - 1) // 2)]))
                        if sec.any("acc", sec.no["acc"][("norm", st, g, hf)] - 1):
                            pe.wait_ge(acc_read, sec.value("acc", sec.no["acc"][("norm", st, g, hf)] - 1))
                        if sec.any("norm", sec.no["norm"][("norm", st, g, hf)] - 1):
                            pe.wait_ge(out_read, sec.value("norm", sec.no["norm"][("norm", st, g, hf)] - 1))
                    for j in range(G):
                        c = P * g + HD * j
                        pe.matmul(ps_acc[HD * j:HD * j + HD, 0, a:HALF], v_sb[:, k, c:c + HD],
                                  probs[:, sec.no["mix"][s] % 2, j, a:HALF],
                                  start=(k == 0), stop=(k == last_tile(st, hf)))

                def sums(s):
                    _, st, g, hf, k, _ = s
                    a = first(st, hf, k)
                    for j in range(G):
                        mm = pe.matmul(ps_acc[HD * j:HD * j + HD, 1, a:HALF], ones32[:],
                                       probs[:, sec.no["mix"][s] % 2, j, a:HALF],
                                       start=(k == 0), stop=(k == last_tile(st, hf)))
                    mm.then_inc(mixed, 1)

                def times_down(hf, j):
                    m = hf * ET + j
                    read(("up", hf, j))
                    if j == 0:
                        pe.wait_ge(acc_read, sec.value("acc", sec.no["acc"][("down", hf)] - 1))
                    for ct in range(CT):
                        mm = pe.matmul(ps_acc[:, ct, :], vals_sb[:, m % RING, P * ct:P * ct + P],
                                       gated[:, m % RING, :], start=(j == 0), stop=(j == ET - 1))
                    mm.then_inc(downed, 1)

                for s in sec.steps:
                    kind = s[0]
                    if kind == "gn":
                        pe.wait_ge(gn_stats, sec.value("gn", sec.no["gn"][s]))
                        filled(pe.matmul(bank(s)[:, 0:2 * CT], block_w[:],
                                         small[:, 0, :, :].rearrange("p k s -> p (k s)"),
                                         start=True, stop=True), s)
                    elif kind == "qk":
                        _, st, g, w, hf = s
                        key = ("lnb", 0, hf) if st else ("split", hf)
                        if g == 0:
                            pe.wait_ge(acts_lo, sec.value("acts", sec.no["acts"][key]))
                        acc = bank(s)
                        m = 4 * st + "qk".index(w)
                        for k in range(CT):
                            mm = split(acc, parts(m, k, P * g, P * g + P),
                                       acts(k, HALF * hf, HALF * hf + HALF), k == 0, k == CT - 1)
                        filled(mm, s)
                    elif kind == "v":
                        _, st, n = s
                        acc = bank(s)
                        for i in range(2):
                            at = (2 * n + i) * P
                            for k in range(CT):
                                mm = split(acc[:, C * i:C * i + C], acts(k, at, at + P),
                                           parts(4 * st + 2, k, 0, C), k == 0, k == CT - 1)
                        filled(mm, s)
                    elif kind == "top":
                        _, st, g, j, i = s
                        if i % PH == 0:
                            for hf in [i // PH] if st else range(NH) if i == 0 else []:
                                n = sec.no[f"stacks{g}{hf}"][("stack", st, g)] if st or g else 0
                                pe.wait_ge(stacked[g][hf][j], sec.value(f"stacks{g}{hf}", n, STACK))
                        acc = bank(s)
                        n_keys = cols(st, i)
                        for c0 in range(0, n_keys, HALF):
                            c1 = min(c0 + HALF, n_keys)
                            diag = st == 1 and c1 == n_keys
                            mm = pe.matmul(acc[:, c0:c1], q_st[0:MID, g, j, P * i:P * i + P],
                                           k_st[0:MID, g, j, c0:c1], start=True, stop=not diag)
                            if diag:
                                mm = pe.matmul(acc[:, c1 - P:c1], ident_bf[:], mask_qk[:], start=False, stop=True)
                        filled(mm, s)
                    elif kind == "row":
                        _, st, g, j, hf = s
                        for u in maxima(s):
                            read(u)
                        acc = bank(s)
                        for i in range(PH * hf, PH * hf + PH):
                            mm = pe.matmul(acc[MID:MID + 1, P * i:P * i + P], tops[:, j, i:i + 1], minus_bf[:],
                                           start=True, stop=True)
                        filled(mm, s)
                    elif kind == "mix":
                        _, st, g, hf, k, wide = s
                        if k == 0:
                            pe.wait_ge(row_ready, sec.value("row", sec.no["row"][("row", st, g, G - 1, hf)]))
                        a = first(st, hf, k)
                        diag = st == 1 and k >= PH * hf
                        per = 2 if wide else 1
                        for n in range(G // per):
                            if n == G // per // 2 and k > 0:
                                times_values(("mix", st, g, hf, k - 1, wide))
                            u = s + (n,)
                            acc = bank(u)
                            for j in range(per * n, per * n + per):
                                at = acc[:, HALF * (j % per):HALF * (j % per) + HALF]
                                mm = pe.matmul(at[:, a:HALF], k_st[0:MID + 1, g, j, P * k:P * k + P],
                                               q_st[0:MID + 1, g, j, HALF * hf + a:HALF * hf + HALF],
                                               start=True, stop=not diag)
                                if diag:
                                    mm = pe.matmul(at[:, a:a + P], ident_bf[:], mask_kq[:], start=False, stop=True)
                            filled(mm, u)
                        if k > 0:
                            sums(("mix", st, g, hf, k - 1, wide))
                    elif kind == "norm":
                        _, st, g, hf = s
                        times_values(last_mix(sec, s))
                        sums(last_mix(sec, s))
                    elif kind == "out":
                        _, st, hf, ct = s
                        pe.wait_ge(att_lo, sec.value("fin", sec.no["fin"][("fin", st, CT - 1, hf)]))
                        acc = bank(s)
                        for k in range(CT):
                            mm = split(acc, parts(4 * st + 3, k, P * ct, P * ct + P),
                                       acts(k, HALF * hf, HALF * hf + HALF), k == 0, k == CT - 1)
                        filled(mm, s)
                    elif kind == "lna":
                        _, ln, hf = s
                        for ct in range(CT):
                            read(("out", ln, hf, ct))
                        acc = bank(s)
                        for k in range(CT):
                            mm = pe.matmul(acc, mean_w[:], x_res[:, k, half(hf)], start=(k == 0), stop=(k == CT - 1))
                        filled(mm, s)
                    elif kind == "lnb":
                        pe.wait_ge(squared, sec.value("lnb", sec.no["lnb"][s]))
                        acc = bank(s)
                        for k in range(CT):
                            mm = pe.matmul(acc, mean_w[:], squares[:, k, :], start=(k == 0), stop=(k == CT - 1))
                        filled(mm, s)
                    elif kind == "logits":
                        pe.wait_ge(xn_ready, sec.value("lnb", sec.no["lnb"][("lnb", 1, NH - 1)]))
                        acc = bank(s)
                        for i in range(TT):
                            for k in range(CT):
                                mm = pe.matmul(acc[:, E * i:E * i + E], xn[:, k, P * i:P * i + P], sel_w[:, k, :],
                                               start=(k == 0), stop=(k == CT - 1))
                        filled(mm, s)
                    elif kind == "turn":
                        pe.wait_ge(gates, sec.value("logits", 0))
                        acc = bank(s)
                        for hf in range(NH):
                            mm = pe.transpose(acc[:, P * hf:P * hf + P],
                                              squares[:, 0, P * hf:P * hf + P],
                                              ident[:])
                        filled(mm, s)
                    elif kind == "up":
                        _, hf, j = s
                        m = hf * ET + j
                        r = m % RING
                        pe.wait_ge(expert_in[r], (sec.value("turn", 0) * (NH * ET // RING) + m // RING + 1) * 16)
                        acc = bank(s)
                        for k in range(CT):
                            mm = pe.matmul(acc, keys_sb[:, r, k, :], xn[:, k, half(hf)],
                                           start=(k == 0), stop=(k == CT - 1))
                        filled(mm, s)
                        if j:
                            times_down(hf, j - 1)
                    elif kind == "down":
                        times_down(s[1], ET - 1)

            pe.wait_ge(consts, N_CONSTS)
            pe.wait_ge(fills, 2)
            pe.wait_ge(weights_hi, 1)
            pe.wait_ge(weights_lo, 1)
            run(pe, emit)

        @block.scalar
        def _(act):
            act.preload_act_table_set("natural_log_exp_and_others")
            staged = probs[:, :, :, :].rearrange("p a g t -> p (a g t)")
            act.wait_ge(weights_in, 64)
            act.copy(w_hi[:, :, :, :].rearrange("p m k c -> p (m k c)"), staged).then_inc(weights_hi, 1)
            act.wait_ge(weights_lo, 1)

            def emit(sec, it):
                def full(u):
                    b, n = sec.bank(u)
                    act.wait_ge(bank_full[b], sec.value(b, n))
                    return (ps_one if b[:3] == "one" else ps_two)[:, int(b[3]), :]

                def read(u):
                    b, n = sec.bank(u)
                    act.wait_ge(bank_read[b], sec.value(b, n))

                def done(ins, u):
                    ins.then_inc(bank_read[sec.bank(u)[0]], 1)

                def inverse_root(out_, var, roots, ready):
                    act.activation(out_, var, ACT.Ln).then_inc(logged, 1)
                    act.wait_ge(logged, roots)
                    act.activation(out_, out_, ACT.Exp, scale=-0.5).then_inc(ready, 1)

                gn_seen = lnb_seen = 0
                for s in sec.steps:
                    kind = s[0]
                    if kind == "gn":
                        gn_seen += 1
                        act.wait_ge(gn_var, sec.value("gn", gn_seen))
                        inverse_root(small[:, 5, :, 0], small[:, 4, :, 0],
                                     sec.value("gn", gn_seen) + sec.value("lnb", lnb_seen), gn_root)
                    elif kind == "split":
                        hf = s[1]
                        act.wait_ge(xt_ready, sec.value("split", sec.no["split"][s]))
                        if sec.name != "first":
                            read(("out", 1, hf, CT - 1))
                        act.copy(act_hi[:, :, half(hf)], xt[:, :, :]).then_inc(acts_hi, 1)
                    elif kind == "qk":
                        _, st, g, w, hf = s
                        acc = full(s)
                        if w == "q":
                            other = 1 - g
                            n = {(0, 0): 2, (0, 1): 0, (1, 0): 1, (1, 1): 1}[(st, g)] if sec.name != "first" else 0
                            for j in range(G):
                                if sec.any(f"stacks{other}{hf}", n):
                                    act.wait_ge(stacked[other][hf][j], sec.value(f"stacks{other}{hf}", n, STACK))
                        m = 4 * st + "qk".index(w)
                        act.activation(nat[:, 2 * "qk".index(w), half(hf)], acc, ACT.Identity,
                                       bias=bias[:, m, g:g + 1]).then_inc(nat_hi_ready, 1)
                    elif kind == "v":
                        _, st, n = s
                        done(act.copy(v_sb[:, 2 * n:2 * n + 2, :].rearrange("p i c -> p (i c)"), full(s)), s)
                        b, number = sec.bank(s)
                        act.wait_ge(bank_read[b], sec.value(b, number))
                        act.sem_inc(v_ready, 1)
                    elif kind == "row":
                        _, st, g, j, hf = s
                        b, n = sec.bank(s)
                        full(s)
                        done(act.copy(q_st[MID:MID + 1, g, j, half(hf)],
                                      ps_two[MID:MID + 1, int(b[3]), half(hf)]), s)
                        act.wait_ge(bank_read[b], sec.value(b, n))
                        act.sem_inc(row_ready, 1)
                    elif kind == "mix":
                        _, st, g, hf, k, wide = s
                        a = first(st, hf, k)
                        n = sec.no["mix"][s]
                        if sec.any("mix", n - 2):
                            act.wait_ge(mixed, sec.value("mix", n - 2))
                        if n <= 2 and sec.name == "body":
                            act.wait_ge(acc_read, sec.value("acc", sec.no["acc"][("down", NH - 1)]))
                        per = 2 if wide else 1
                        for i in range(G // per):
                            acc = full(s + (i,)).rearrange("p (g t) -> p g t", g=per)
                            done(act.activation(probs[:, n % 2, per * i:per * i + per, a:HALF], acc[:, :, a:HALF],
                                                ACT.Exp, scale=SCALE), s + (i,))
                    elif kind == "norm":
                        _, st, g, hf = s
                        act.wait_ge(mixed, sec.value("mix", sec.no["mix"][last_mix(sec, s)]))
                        if sec.any("norm", sec.no["norm"][s] - 1):
                            act.wait_ge(att_ready, sec.value("norm", sec.no["norm"][s] - 1))
                        act.copy(o_sb[:], ps_acc[:, 0, :]).then_inc(out_read, 1)
                    elif kind == "fin":
                        _, st, g, hf = s
                        act.wait_ge(att_ready, sec.value("norm", sec.no["norm"][("norm",) + s[1:]]))
                        act.activation(act_hi[:, g, half(hf)], rsum[:], ACT.Identity,
                                       bias=bias[:, 4 * st + 2, g:g + 1]).then_inc(att_hi, 1)
                    elif kind == "lna":
                        _, ln, hf = s
                        read(s)
                        n = lnb_seen
                        if sec.any("lnb", n):
                            act.wait_ge(squared_read, sec.value("lnb", n))
                        act.activation(squares[:, :, :], xn[:, :, half(hf)], ACT.Square).then_inc(squared, 1)
                    elif kind == "lnb":
                        _, ln, hf = s
                        lnb_seen += 1
                        read(s)
                        if sec.any("lnb", lnb_seen - 1):
                            act.wait_ge(xn_ready, sec.value("lnb", lnb_seen - 1))
                        inverse_root(rstd[:], var_sb[:],
                                     sec.value("gn", gn_seen) + sec.value("lnb", lnb_seen), ln_root)
                        if ln == 0:
                            act.wait_ge(xn_ready, sec.value("lnb", lnb_seen))
                            act.copy(act_hi[:, :, half(hf)], xn[:, :, half(hf)]).then_inc(acts_hi, 1)
                    elif kind == "logits":
                        done(act.activation(w_tok, full(s)[:, 0:TT * E].rearrange("p (i e) -> p i e", e=E),
                                            ACT.Exp, scale=-1.0), s)

            run(act, emit)

        @block.vector
        def _(dve):
            staged = probs[:, :, :, :].rearrange("p a g t -> p (a g t)")
            dve.memset(f(k_st[MID:MID + 1, :, :, :]), 1.0).then_inc(fills, 1)
            dve.memset(pad_sel[:], -1.0).then_inc(fills, 1)
            dve.wait_ge(weights_hi, 1)
            dve.wait_ge(weights_in, 64)
            dve.tensor_tensor(w_lo[:, :, :, :].rearrange("p m k c -> p (m k c)"), staged,
                              f(w_hi[:, :, :, :].rearrange("p m k c -> p (m k c)")),
                              ALU.subtract).then_inc(weights_lo, 1)
            dve.wait_ge(consts, N_CONSTS)
            dve.wait_ge(weights_lo, 1)
            dve.wait_ge(fills, 2)

            def emit(sec, it):
                def full(u):
                    b, n = sec.bank(u)
                    dve.wait_ge(bank_full[b], sec.value(b, n))
                    return (ps_one if b[:3] == "one" else ps_two)[:, int(b[3]), :]

                def read(u):
                    b, n = sec.bank(u)
                    dve.wait_ge(bank_read[b], sec.value(b, n))

                def done(ins, u):
                    ins.then_inc(bank_read[sec.bank(u)[0]], 1)

                links = [0]

                def link(ins):
                    links[0] += 1
                    ins.then_inc(linked, 1)
                    dve.wait_ge(linked, sec.value("link", links[0]))

                def refine(y, var, tmp):
                    link(dve.tensor_tensor(tmp, var, y, ALU.mult))
                    link(dve.tensor_tensor(tmp, tmp, y, ALU.mult))
                    link(dve.tensor_scalar(tmp, tmp, -0.5, 1.5, ALU.mult, ALU.add))
                    link(dve.tensor_tensor(y, y, tmp, ALU.mult))

                for s in sec.steps:
                    kind = s[0]
                    if kind == "gn":
                        n = sec.no["gn"][s]
                        dve.wait_ge(x_loaded, sec.value("gn", n, 16))
                        for k in range(CT):
                            for hf in range(NH):
                                ins = dve.bn_stats(st6[:, k, hf, :], x_in[:, k, half(hf)])
                        link(ins)
                        dve.sem_inc(passed, 1)
                        for k in range(CT):
                            ins = dve.bn_aggr(mv[:, k, :], st6[:, k, :, :].rearrange("p h s -> p (h s)"))
                        link(ins)
                        dve.tensor_copy(small[:, 0, :, 0], mv[:, :, 0])
                        link(dve.tensor_tensor(small[:, 1, :, 0], mv[:, :, 0], mv[:, :, 0], ALU.mult))
                        dve.tensor_tensor(small[:, 0, :, 1], small[:, 1, :, 0], mv[:, :, 1],
                                          ALU.add).then_inc(gn_stats, 1)
                        acc = full(s)
                        done(dve.tensor_copy(small[:, 2, :, :].rearrange("p k s -> p (k s)"), acc[:, 0:2 * CT]), s)
                        read(s)
                        link(dve.tensor_tensor(small[:, 3, :, 0], small[:, 2, :, 0], small[:, 2, :, 0], ALU.mult))
                        link(dve.tensor_tensor(small[:, 3, :, 1], small[:, 2, :, 1], small[:, 3, :, 0],
                                               ALU.subtract))
                        dve.tensor_scalar(small[:, 4, :, 0], small[:, 3, :, 1], 1e-5, None,
                                          ALU.add).then_inc(gn_var, 1)
                        dve.wait_ge(gn_root, sec.value("gn", n))
                        refine(small[:, 5, :, 0], small[:, 4, :, 0], small[:, 5, :, 1])
                        link(dve.tensor_tensor(small[:, 6, :, 0], small[:, 5, :, 0], gnw[:, 0, :], ALU.mult))
                        dve.tensor_tensor(small[:, 6, :, 1], small[:, 2, :, 0], small[:, 6, :, 0],
                                          ALU.mult).then_inc(linked, 1)
                        links[0] += 1
                        dve.wait_ge(linked, sec.value("link", links[0]))
                        dve.tensor_tensor(small[:, 7, :, 0], gnw[:, 1, :], small[:, 6, :, 1],
                                          ALU.subtract).then_inc(offsets, 1)
                        dve.wait_ge(offsets, sec.value("gn", n))
                    elif kind == "split":
                        hf = s[1]
                        n = sec.no["split"][s]
                        if sec.any("acts", sec.no["acts"][s] - 1):
                            dve.wait_ge(acts_lo, sec.value("acts", sec.no["acts"][s] - 1))
                        for k in range(CT):
                            ins = dve.tensor_scalar(xt[:, k, :], x_in[:, k, half(hf)], small[:, 6, k, 0:1],
                                                    small[:, 7, k, 0:1], ALU.mult, ALU.add)
                        ins.then_inc(xt_ready, 1)
                        dve.wait_ge(xt_ready, sec.value("split", n))
                        dve.wait_ge(acts_hi, sec.value("acts", sec.no["acts"][s]))
                        dve.tensor_tensor(act_lo[:, :, half(hf)], xt[:, :, :], f(act_hi[:, :, half(hf)]),
                                          ALU.subtract).then_inc(acts_lo, 1)
                    elif kind == "qk":
                        _, st, g, w, hf = s
                        m, n = 4 * st + "qk".index(w), 2 * "qk".index(w)
                        acc = full(s)
                        dve.wait_ge(nat_hi_ready, sec.value("qk", sec.no["qk"][s]))
                        done(dve.scalar_tensor_tensor(out=nat[:, n + 1, half(hf)], in0=acc, scalar=bias[:, m, g:g + 1],
                                                      in1=f(nat[:, n, half(hf)]), op0=ALU.add,
                                                      op1=ALU.subtract), s)
                    elif kind == "top":
                        _, st, g, j, i = s
                        acc = full(s)
                        if i % PH == 0:
                            if sec.any("row", sec.no["row"][("row", st, g, j, i // PH)] - G):
                                dve.wait_ge(row_ready, sec.value("row", sec.no["row"][("row", st, g, j, i // PH)] - G))
                        done(dve.reduce_max(tops[:, j, i:i + 1], acc[:, 0:cols(st, i)], AX_X), s)
                    elif kind == "norm":
                        _, st, g, hf = s
                        dve.wait_ge(mixed, sec.value("mix", sec.no["mix"][last_mix(sec, s)]))
                        if sec.any("fin", sec.no["norm"][s] - 1):
                            dve.wait_ge(att_lo, sec.value("fin", sec.no["norm"][s] - 1))
                        dve.tensor_copy(rsum[:], ps_acc[:, 1, :]).then_inc(acc_read, 1)
                        dve.wait_ge(acc_read, sec.value("acc", sec.no["acc"][s]))
                        link(dve.reciprocal(rsum[:], rsum[:]))
                        dve.wait_ge(out_read, sec.value("norm", sec.no["norm"][s]))
                        dve.tensor_tensor(rsum[:], o_sb[:], rsum[:], ALU.mult).then_inc(att_ready, 1)
                    elif kind == "fin":
                        _, st, g, hf = s
                        n = sec.no["fin"][s]
                        dve.wait_ge(att_ready, sec.value("norm", n))
                        dve.wait_ge(att_hi, sec.value("fin", n))
                        dve.scalar_tensor_tensor(out=act_lo[:, g, half(hf)], in0=rsum[:],
                                                 scalar=bias[:, 4 * st + 2, g:g + 1],
                                                 in1=f(act_hi[:, g, half(hf)]),
                                                 op0=ALU.add, op1=ALU.subtract).then_inc(att_lo, 1)
                    elif kind == "out":
                        _, st, hf, ct = s
                        acc = full(s)
                        before = x_res if st else x_in
                        if st == 0 and sec.name == "body":
                            dve.wait_ge(stored[hf], sec.value("turn", 1, 16))
                        done(dve.scalar_tensor_tensor(out=x_res[:, ct, half(hf)], in0=acc,
                                                      scalar=bias[:, 4 * st + 3, ct:ct + 1],
                                                      in1=before[:, ct, half(hf)], op0=ALU.add, op1=ALU.add), s)
                    elif kind == "lna":
                        _, ln, hf = s
                        acc = full(s)
                        for ct in range(CT):
                            read(("out", ln, hf, ct))
                        link(dve.tensor_tensor(xn[:, 0, half(hf)], x_res[:, 0, half(hf)], acc, ALU.subtract))
                        done(dve.tensor_tensor(xn[:, 1, half(hf)], x_res[:, 1, half(hf)], acc, ALU.subtract), s)
                    elif kind == "lnb":
                        _, ln, hf = s
                        acc = full(s)
                        done(dve.tensor_scalar(var_sb[:], acc, 1e-5, None, ALU.add), s)
                        read(s)
                        n = sec.no["lnb"][s]
                        dve.wait_ge(ln_root, sec.value("lnb", n))
                        refine(rstd[:], var_sb[:], rtmp)
                        dve.sem_inc(squared_read, 1)
                        link(dve.tensor_tensor(xn[:, 0, half(hf)], xn[:, 0, half(hf)], rstd[:], ALU.mult))
                        dve.tensor_tensor(xn[:, 1, half(hf)], xn[:, 1, half(hf)], rstd[:],
                                          ALU.mult).then_inc(xn_ready, 1)
                        if ln == 0:
                            dve.wait_ge(acts_hi, sec.value("acts", sec.no["acts"][s]))
                            dve.tensor_tensor(act_lo[:, :, half(hf)], xn[:, :, half(hf)], f(act_hi[:, :, half(hf)]),
                                              ALU.subtract).then_inc(acts_lo, 1)
                    elif kind == "logits":
                        read(s)
                        link(dve.tensor_scalar(w_tok, w_tok, 1.0, None, ALU.add))
                        link(dve.reciprocal(pad_sel[:, :, 0:E], w_tok))
                        dve.sem_inc(passed, 1)
                        for i in range(TT):
                            ins = dve.max(top8[:, i, :], pad_sel[:, i, 0:E])
                        link(ins)
                        link(dve.memset(top8[:, :, 2:8], -1.0))
                        dve.sem_inc(passed, 1)
                        for i in range(TT):
                            ins = dve.match_replace(rest[:, i, :], top8[:, i, :], pad_sel[:, i, :], 0.0)
                        link(ins)
                        dve.tensor_tensor(w_tok, pad_sel[:, :, 0:E], rest[:, :, 0:E],
                                          ALU.subtract).then_inc(gates, 1)
                    elif kind == "turn":
                        done(dve.tensor_copy(w_turn[:].rearrange("p h t -> p (h t)"), full(s)[:, 0:NH * P]), s)
                    elif kind == "up":
                        _, hf, j = s
                        m = hf * ET + j
                        acc = full(s)
                        r = m % RING
                        dve.wait_ge(gate_in[r], (sec.value("turn", 0) * (NH * ET // RING) + m // RING + 1) * 16)
                        if sec.any("up", m + 1 - RING):
                            dve.wait_ge(downed, sec.value("up", m + 1 - RING))
                        done(dve.scalar_tensor_tensor(out=gated[:, r, :], in0=acc, scalar=0.0,
                                                      in1=gate_bc[:, r, :], op0=ALU.max, op1=ALU.mult), s)
                    elif kind == "down":
                        hf = s[1]
                        dve.wait_ge(downed, sec.value("up", (hf + 1) * ET))
                        dve.tensor_tensor(x_res[:, 0, half(hf)], ps_acc[:, 0, :], x_res[:, 0, half(hf)], ALU.add)
                        dve.tensor_tensor(x_res[:, 1, half(hf)], ps_acc[:, 1, :], x_res[:, 1, half(hf)],
                                          ALU.add).then_inc(acc_read, 1)
                assert links[0] == len(sec.no.get("link", {})), (sec.name, links[0])

            run(dve, emit)


def next_batch(it, batches):
    return it + 1 if isinstance(it, int) else (it + 1) % batches


def kernel(**inputs):
    import concourse.bacc as bacc
    from concourse.bass_utils import run_bass_kernel_spmd

    a = {n: np.asarray(v) for n, v in inputs.items()}
    B, C, Hh, Ww = a["x"].shape
    T = Hh * Ww
    CT = C // P
    heads = 8
    ch = C // heads
    qkv = a["L0_conv_qkv_w"].reshape(heads, 3, ch, C)
    qkv_b = a["L0_conv_qkv_b"].reshape(heads, 3, ch)
    mats = [qkv[:, n].reshape(C, C).T for n in range(3)] + [a["L0_conv_proj_w"].T]
    mats += [a["L1_attn_W_" + n] for n in "QKVO"]
    vecs = [qkv_b[:, n].reshape(C) for n in range(3)] + [a["L0_conv_proj_b"]]
    vecs += [a["L1_attn_b_" + n] for n in "QKVO"]
    keys = a["L1_ffn_keys"]
    E, _, H = keys.shape
    ET = E * H // P

    def by_partition(m):
        return np.moveaxis(m.reshape(m.shape[:-1] + (CT, P)), -1, 0)

    arrays = {
        "x_in_dram": a["x"].reshape(B, C, T),
        "mats_dram": np.stack(mats).reshape(8, CT, P, C).transpose(2, 0, 1, 3),
        "vecs_dram": by_partition(np.stack(vecs)),
        "norm_dram": by_partition(np.stack([a["L0_conv_norm_w"], a["L0_conv_norm_b"]])),
        "sel_dram": a["L1_ffn_expert_sel"].T.reshape(CT, P, E).transpose(1, 0, 2),
        "experts_dram": np.concatenate(
            [keys.transpose(1, 0, 2).reshape(CT, P, ET, P).transpose(2, 1, 0, 3).reshape(ET, P, C),
             a["L1_ffn_values"].reshape(ET, P, C)], axis=2),
    }
    arrays = {n: np.ascontiguousarray(v) for n, v in arrays.items()}
    nc = bacc.Bacc("TRN2", target_bir_lowering=False, num_devices=1)
    args = [nc.dram_tensor(n, v.shape, mybir.dt.from_np(v.dtype), kind="ExternalInput").ap()
            for n, v in arrays.items()]
    out = nc.dram_tensor("out_dram", (B, C, T), F32, kind="ExternalOutput").ap()
    w_dram = nc.dram_tensor("gates_dram", (E, T), F32, kind="Internal").ap()
    bass_hybrid_kernel(nc, *args, out, w_dram)
    r = run_bass_kernel_spmd(nc, [arrays], core_ids=[0])
    return r.results[0]["out_dram"].reshape(B, C, Hh, Ww)
```

```python
from contextlib import ExitStack

import numpy as np

import concourse.bass as bass
from concourse import mybir

ACT = mybir.ActivationFunctionType
ALU = mybir.AluOpType
AX_X = mybir.AxisListType.X
F32 = mybir.dt.float32
F32R = mybir.dt.float32r
BF16 = mybir.dt.bfloat16

P = 128
HALF = 512
HEADS_PER_GROUP = 4
MASKED = -1.0e30


def spread(main, side):
    out, done = [], 0
    for n, step in enumerate(main):
        out.append(step)
        upto = len(side) * (n + 1) // len(main)
        out += side[done:upto]
        done = upto
    return out


def rows_later(steps, by=2):
    out, held = [], []
    for s in steps:
        if s[0] == "row":
            held.append([s, by])
            continue
        out.append(s)
        for h in held:
            h[1] -= 1
        out += [h[0] for h in held if h[1] == 0]
        held = [h for h in held if h[1] > 0]
    return out + [h[0] for h in held]


class Steps:

    def __init__(self, tiles, halves, channel_tiles, expert_tiles):
        self.tiles, self.halves, self.groups, self.experts = tiles, halves, channel_tiles, expert_tiles

    def qk(self, st, g, halves=None):
        out = []
        for hf in range(self.halves) if halves is None else halves:
            out += [("qk", st, g, "q", hf), ("qk", st, g, "k", hf), ("stack", st, g, hf)]
        return out

    def v(self, st):
        return [("v", st, n) for n in range(self.tiles // 2)]

    def top(self, st, g, hf):
        per_half = self.tiles // self.halves
        out = []
        for j in range(HEADS_PER_GROUP):
            out += [("top", st, g, j, i) for i in range(per_half * hf, per_half * (hf + 1))] + [("row", st, g, j, hf)]
        return out

    def mix(self, st, g, hf, wide):
        last = self.tiles // self.halves * (hf + 1) if st else self.tiles
        return [("mix", st, g, hf, k, wide) for k in range(last)]

    def out(self, st, hf):
        return [("out", st, hf, ct) for ct in range(self.groups)]

    def first(self):
        return [("stats",), ("gn",), ("split", 0), ("split", 1)] + self.qk(0, 0) + self.v(0)[:2]

    def experts_of(self, tops):
        ups = [("up", hf, j) for hf in range(self.halves) for j in range(self.experts)]
        steps = spread(ups, tops) if tops else ups
        at = steps.index(("up", 0, self.experts - 1)) + 1
        behind = at + 2 if tops else at
        return steps[:at] + [("lower", 0)] + steps[at:behind] + [("down", 0)] + steps[behind:] + [("lower", 1)]

    def batch(self, experts):
        tops = rows_later(self.top(0, 0, 0) + self.top(0, 0, 1) + self.top(0, 1, 0) + self.top(0, 1, 1))
        if experts:
            steps = self.qk(0, 1, [0]) + [("logits",)] + self.v(0)[2:] + self.qk(0, 1, [1]) + [("inputs",)]
            steps += tops[:3] + [("turn",)] + tops[3:10] + self.experts_of(tops[10:])
        else:
            steps = self.v(0)[2:] + self.qk(0, 1) + tops
        a, b, c, d = (self.mix(0, g, hf, True) for hf in (0, 1) for g in (0, 1))
        steps += a[:1] + ([("down", 1)] if experts else []) + a[1:]
        steps += b[:1] + [("norm", 0, 0, 0), b[1], ("div", 0, 0, 0), b[2], ("fin", 0, 0, 0)] + b[3:]
        steps += c[:1] + [("norm", 0, 1, 0), c[1], ("div", 0, 1, 0), c[2], ("fin", 0, 1, 0), c[3]] + self.out(0, 0)
        steps += [c[4], ("lna", 0, 0), c[5], ("lnb", 0, 0), c[6], c[7], ("parts", 0)]
        steps += d[:1] + [("norm", 0, 0, 1), d[1]] + self.qk(1, 0, [0]) + [("div", 0, 0, 1), d[2], ("fin", 0, 0, 1)]
        t = rows_later(self.top(1, 0, 0))
        steps += d[3:5] + spread(d[5:8] + self.v(1)[:2], t)
        e, f, g, h = (self.mix(1, g, hf, hf == g) for hf in (0, 1) for g in (0, 1))
        t = rows_later(self.top(1, 1, 0))
        steps += e[:1] + [("norm", 0, 1, 1)] + self.qk(1, 1, [0]) + [("div", 0, 1, 1), e[1], e[2], ("fin", 0, 1, 1)]
        steps += [e[3]] + t[:3] + self.out(0, 1) + t[3:8] + [("lna", 0, 1)] + t[8:]
        steps += f[:1] + [("norm", 1, 0, 0), ("lnb", 0, 1), f[1], f[2], ("parts", 1), ("div", 1, 0, 0)]
        steps += self.qk(1, 0, [1]) + [("fin", 1, 0, 0)] + self.v(1)[2:]
        steps += spread([f[3]] + self.qk(1, 1, [1]), rows_later(self.top(1, 0, 1)))
        m = [g[1], ("div", 1, 1, 0), g[2], ("fin", 1, 1, 0)] + g[3:]
        t = rows_later(self.top(1, 1, 1))
        steps += g[:1] + [("norm", 1, 1, 0)] + spread(m[:-1], t[:-1]) + [m[-1], t[-1]]
        steps += h[:1] + [("norm", 1, 0, 1), h[1], ("div", 1, 0, 1), h[2], ("fin", 1, 0, 1), ("stats",), h[3]]
        steps += self.out(1, 0) + [("gn",), h[4], ("lna", 1, 0), h[5], ("split", 0), ("lnb", 1, 0), h[6], h[7]]
        steps += [("norm", 1, 1, 1), ("div", 1, 1, 1)] + self.qk(0, 0, [0]) + [("fin", 1, 1, 1)] + self.v(0)[:2]
        steps += self.out(1, 1)
        steps += [("split", 1), ("lna", 1, 1)] + self.qk(0, 0, [1]) + [("lnb", 1, 1)]
        return steps

    def last(self):
        return [("logits",), ("inputs",), ("turn",)] + self.experts_of([]) + [("down", 1)]


LINKS = {"stats": 3, "gn": 8, "div": 2, "lna": 1, "lnb": 5, "logits": 5}
N_CONSTS = 15


def events(steps):
    kinds = {}

    def add(kind, key):
        kinds.setdefault(kind, {})[key] = len(kinds.get(kind, {})) + 1

    turn = {"one": 0, "two": 0}

    def use(bank, key):
        add(f"{bank}{turn[bank] % 2}", key)
        turn[bank] += 1

    for s in steps:
        kind = s[0]
        add(kind, s)
        if kind in ("gn", "qk", "v", "out", "lna", "lnb", "logits", "turn", "up"):
            use("one", s)
        if kind == "mix":
            for n in range(2 if s[5] else HEADS_PER_GROUP):
                use("two" if s[5] else "one", s + (n,))
        if kind in ("top", "row"):
            use("two", s)
        if kind in ("norm", "down"):
            add("acc", s)
        if kind in ("split", "parts", "inputs"):
            add("acts", s)
        if kind == "stack":
            add(f"stacks{s[2]}{s[3]}", s[:3])
        for n in range(LINKS.get(kind, 0)):
            add("link", s + (n,))
    return kinds


def bass_hybrid_kernel(nc: bass.Bass, x, mats, vecs, norm_wb, sel_t, experts, out, w_dram):
    B, C, T = x.shape
    E = sel_t.shape[2]
    H = experts.shape[0] * P // E
    CT = C // P
    NH = T // HALF
    TT = T // P
    PH = HALF // P
    G = HEADS_PER_GROUP
    HD = P // G
    MID = 3 * HD
    ET = E * H // P
    EPT = P // H
    RING = 4
    SCALE = float(HD) ** -0.5
    NORM_GROUP = C // 32
    STACK = 16 * 3
    assert NH == 2 and ET * NH % RING == 0 and 4 * C == T

    plan = Steps(TT, NH, CT, ET)
    SECTIONS = {"first": plan.first(), "head": plan.batch(False), "body": plan.batch(True), "last": plan.last()}
    EVENTS = {name: events(steps) for name, steps in SECTIONS.items()}

    BEFORE = {"first": [], "head": ["first"], "body": ["first", "head"], "last": ["first", "head"]}

    class Section:

        def __init__(self, name, it=None):
            self.name, self.it = name, it
            self.steps, self.no = SECTIONS[name], EVENTS[name]

        def total(self, name, kind):
            return len(EVENTS[name].get(kind, {}))

        def value(self, kind, n, each=1):
            n += sum(self.total(b, kind) for b in BEFORE[self.name])
            if self.name == "body":
                return ((self.it - 1) * self.total("body", kind) + n) * each
            if self.name == "last":
                return ((B - 1) * self.total("body", kind) + n) * each
            return n * each

        def any(self, kind, n):
            value = n + sum(self.total(b, kind) for b in BEFORE[self.name])
            return value + ((B - 1) * self.total("body", kind) if self.name == "last" else 0) > 0

        def bank(self, u):
            return next((b, self.no[b][u]) for b in ("one0", "one1", "two0", "two1") if u in self.no.get(b, {}))

    def cols(st, i):
        return P * (i + 1) if st else T

    def first(st, hf, k):
        return max(0, P * (k - PH * hf)) if st else 0

    def last_tile(st, hf):
        return (PH * (hf + 1) if st else TT) - 1

    def last_mix(sec, s):
        _, st, g, hf = s
        return next(m for m in sec.no["mix"] if m[1:5] == (st, g, hf, last_tile(st, hf)))

    def half(hf):
        return slice(HALF * hf, HALF * hf + HALF)

    with ExitStack() as ctx:
        def sb(name, shape, dt=F32):
            return ctx.enter_context(nc.sbuf_tensor(name, shape, dt))

        def sem(name):
            return ctx.enter_context(nc.semaphore(name))

        w_hi = sb("w_hi", [P, 8, CT, C], F32R)
        w_lo = sb("w_lo", [P, 8, CT, C], F32R)
        bias = sb("bias", [P, 8, CT])
        gnw = sb("gnw", [P, 2, CT])
        sel_w = sb("sel_w", [P, CT, E])
        ident = sb("ident", [P, P])
        ident_bf = sb("ident_bf", [P, P], BF16)
        minus_bf = sb("minus_bf", [P, P], BF16)
        mask_qk = sb("mask_qk", [P, P], BF16)
        mask_kq = sb("mask_kq", [P, P], BF16)
        mean_w = sb("mean_w", [P, P])
        block_w = sb("block_w", [P, P])
        ones32 = sb("ones32", [P, HD])

        x_in = sb("x_in", [P, CT, T])
        x_res = sb("x_res", [P, CT, T])
        xt = sb("xt", [P, CT, HALF])
        xn = sb("xn", [P, CT, T])
        act_hi = sb("act_hi", [P, CT, T], F32R)
        act_lo = sb("act_lo", [P, CT, T], F32R)
        nat = sb("nat", [P, 4, T], F32R)
        stacks = sb("stacks", [P, 2, CT, G, T], F32R)
        q_st, k_st = stacks[:, 0, :, :, :], stacks[:, 1, :, :, :]
        v_sb = sb("v_sb", [P, TT, C])
        probs = sb("probs", [P, 2, G, HALF])
        squares = sb("squares", [P, CT, HALF])
        tops = sb("tops", [P, G, TT], BF16)
        rsum = sb("rsum", [P, HALF])
        o_sb = sb("o_sb", [P, HALF])
        var_sb = sb("var_sb", [P, HALF])
        rstd = sb("rstd", [P, HALF])
        st6 = sb("st6", [P, CT, NH, 6])
        mv = sb("mv", [P, CT, 2])
        small = sb("small", [P, 8, CT, 2])
        expert_sb = sb("expert_sb", [P, RING, CT * P + C])
        pad_sel = sb("pad_sel", [P, TT, E + 8])
        top8 = sb("top8", [P, TT, 8])
        w_turn = sb("w_turn", [P, NH, P])
        rtmp = squares[:, 0, :]
        w_tok = squares[:, 0, 0:TT * E].rearrange("p (i e) -> p i e", e=E)
        rest = squares[:, 1, 0:TT * (E + 8)].rearrange("p (i e) -> p i e", e=E + 8)
        gated = probs[:, 0, :, :]
        keys_parts = nat[:, 0, :].rearrange("p (r c) -> p r c", r=4)
        vals_parts = nat[:, 1, :].rearrange("p (r c) -> p r c", r=4)
        gated_hi = nat[:, 2, :].rearrange("p (r t) -> p r t", r=2)
        gated_lo = nat[:, 3, :].rearrange("p (r t) -> p r t", r=2)
        gate_bc = probs[:, 1, :, :]

        ps_two = ctx.enter_context(nc.psum_tensor("ps_two", [P, 2, T], F32))
        ps_one = ctx.enter_context(nc.psum_tensor("ps_one", [P, 2, HALF], F32))
        ps_acc = ctx.enter_context(nc.psum_tensor("ps_acc", [P, 2, HALF], F32))

        passed = sem("passed")
        passed_too = sem("passed_too")
        consts = sem("consts")
        fills = sem("fills")
        weights_in = sem("weights_in")
        weights_hi = sem("weights_hi")
        weights_lo = sem("weights_lo")
        x_loaded = sem("x_loaded")
        bank_full = {b: sem(f"{b}_full") for b in ("one0", "one1", "two0", "two1")}
        bank_read = {b: sem(f"{b}_read") for b in ("one0", "one1", "two0", "two1")}
        squared_read = sem("squared_read")
        offsets = sem("offsets")
        linked = sem("linked")
        gn_stats = sem("gn_stats")
        gn_var = sem("gn_var")
        gn_root = sem("gn_root")
        xt_ready = sem("xt_ready")
        logged = sem("logged")
        inverse = sem("inverse")
        ln_root = sem("ln_root")
        xn_ready = sem("xn_ready")
        acts_hi = sem("acts_hi")
        acts_lo = sem("acts_lo")
        nat_hi_ready = sem("nat_hi_ready")
        stacked = [[[sem(f"stacked{g}_{hf}_{j}") for j in range(G)] for hf in range(NH)] for g in range(CT)]
        v_ready = sem("v_ready")
        row_ready = sem("row_ready")
        mixed = sem("mixed")
        acc_read = sem("acc_read")
        out_read = sem("out_read")
        att_ready = sem("att_ready")
        att_hi = sem("att_hi")
        att_lo = sem("att_lo")
        squared = sem("squared")
        gates = sem("gates")
        gates_out = sem("gates_out")
        gate_in = [sem(f"gate_in{n}") for n in range(RING)]
        expert_in = [sem(f"expert_in{n}") for n in range(RING)]
        keys_up = sem("keys_up")
        keys_down = sem("keys_down")
        vals_up = sem("vals_up")
        vals_down = sem("vals_down")
        gated_up = sem("gated_up")
        gated_down = sem("gated_down")
        downed = sem("downed")
        stored = [sem(f"stored{hf}") for hf in range(NH)]

        def f(ap):
            return ap.bitcast(F32)

        def run(eng, emit):
            emit(Section("first"), None)
            emit(Section("head"), 0)
            with eng.Fori(1, B) as it:
                emit(Section("body", it), it)
            emit(Section("last"), B)

        block = ctx.enter_context(nc.Block())

        @block.sync
        def _(sp):
            sp.dma_start(x_in[:, :, :], x[0].rearrange("(k p) t -> p k t", p=P)).then_inc(x_loaded, 16)
            sp.dma_start(probs[:, :, :, :].rearrange("p a g t -> p (a g t)"),
                         mats.rearrange("p m k c -> p (m k c)")).then_inc(weights_in, 16)
            sp.dma_start(bias[:, :, :], vecs).then_inc(weights_in, 16)
            sp.dma_start(gnw[:, :, :], norm_wb).then_inc(weights_in, 16)
            sp.dma_start(sel_w[:, :, :], sel_t).then_inc(weights_in, 16)

            def emit(sec, it):
                def hold(semaphore, kind, n, each=1):
                    sp.wait_ge(semaphore, sec.value(kind, n, each))
                    sp.sem_inc(passed, 1)

                def read(u):
                    b, n = sec.bank(u)
                    hold(bank_read[b], b, n)

                for s in sec.steps:
                    if s[0] == "stack":
                        _, st, g, hf = s
                        read(("qk", st, g, "q", hf))
                        read(("qk", st, g, "k", hf))
                        if st:
                            hold(acc_read, "acc", sec.no["acc"][("norm", 0, g, NH - 1)])
                        elif g == 0 and sec.name != "first":
                            hold(acc_read, "acc", sec.no["acc"][("norm", 1, g, NH - 1)])
                        elif sec.name == "body":
                            hold(acc_read, "acc", 0)
                        for j in range(G):
                            rows = slice(HD * j, HD * j + HD)
                            for quad, pair in enumerate((slice(0, 4, 2), slice(0, 4, 3), slice(1, 3, 1))):
                                sp.dma_start(f(stacks[HD * quad:HD * quad + HD, :, g, j, half(hf)]),
                                             f(nat[rows, pair, half(hf)])).then_inc(stacked[g][hf][j], 16)
                    if s == ("out", 0, NH - 1, CT - 1):
                        read(s)
                        sp.dma_start(x_in[:, :, :],
                                     x[bass.ds(next_batch(it, B), 1)].rearrange("a (k p) t -> p (a k) t", p=P)
                                     ).then_inc(x_loaded, 16)
                    if s[0] == "turn":
                        read(s)
                        for i in range(TT):
                            sp.dma_start(w_dram[:, P * i:P * i + P],
                                         w_turn[E * (i % PH):E * (i % PH) + E, i // PH, :]).then_inc(gates_out, 16)
                    if s[0] == "down":
                        hf = s[1]
                        hold(acc_read, "acc", sec.no["acc"][s])
                        where = out[B - 1:B] if sec.name == "last" else out[bass.ds(it - 1, 1)]
                        sp.dma_start(where.rearrange("a (k p) t -> p (a k) t", p=P)[:, :, half(hf)],
                                     x_res[:, :, half(hf)]).then_inc(stored[hf], 16)

            run(sp, emit)
            last = Section("last")
            sp.wait_ge(gates_out, last.value("turn", 1, 16 * TT))
            for hf in range(NH):
                sp.wait_ge(stored[hf], last.value("turn", 1, 16))

        @block.gpsimd
        def _(pool):
            pool.memset(ident[:], 0.0).then_inc(consts, 1)
            pool.memset(ident_bf[:], 0.0).then_inc(consts, 1)
            pool.memset(minus_bf[:], 0.0).then_inc(consts, 1)
            pool.memset(mask_qk[:], 0.0).then_inc(consts, 1)
            pool.memset(mask_kq[:], 0.0).then_inc(consts, 1)
            pool.memset(block_w[:], 1.0 / NORM_GROUP).then_inc(consts, 1)
            pool.memset(mean_w[:], 1.0 / C).then_inc(consts, 1)
            pool.memset(ones32[:], 1.0).then_inc(consts, 1)
            pool.wait_ge(consts, 8)
            for m, value in ((ident, 1.0), (ident_bf, 1.0), (minus_bf, -1.0)):
                pool.affine_select(out=m[:], in_=m[:], compare_op=ALU.not_equal, fill=value, base=0,
                                   pattern=[[-1, P]], channel_multiplier=1).then_inc(consts, 1)
            pool.affine_select(out=mask_qk[:], in_=mask_qk[:], compare_op=ALU.is_ge, fill=MASKED, base=0,
                               pattern=[[-1, P]], channel_multiplier=1).then_inc(consts, 1)
            pool.affine_select(out=mask_kq[:], in_=mask_kq[:], compare_op=ALU.is_ge, fill=MASKED, base=0,
                               pattern=[[1, P]], channel_multiplier=-1).then_inc(consts, 1)
            blocks = block_w[:].rearrange("p (n e) -> p n e", e=NORM_GROUP)
            pool.affine_select(out=blocks, in_=blocks, compare_op=ALU.is_ge, fill=0.0, base=0,
                               pattern=[[-NORM_GROUP, P // NORM_GROUP], [0, NORM_GROUP]],
                               channel_multiplier=1).then_inc(consts, 1)
            pool.wait_ge(consts, 14)
            pool.affine_select(out=blocks, in_=blocks, compare_op=ALU.is_ge, fill=0.0, base=NORM_GROUP - 1,
                               pattern=[[NORM_GROUP, P // NORM_GROUP], [0, NORM_GROUP]],
                               channel_multiplier=-1).then_inc(consts, 1)

            def emit(sec, it):
                def hold(semaphore, kind, n, each=1):
                    pool.wait_ge(semaphore, sec.value(kind, n, each))
                    pool.sem_inc(passed_too, 1)

                def load_expert(m):
                    pool.dma_start(expert_sb[:, m % RING, :], experts[m % ET]).then_inc(expert_in[m % RING], 16)

                def load_gates(m):
                    hf, j = divmod(m, ET)
                    row = w_dram[EPT * j:EPT * j + EPT, half(hf)]
                    pool.dma_start(gate_bc[:, m % RING, :],
                                   bass.AP(row.tensor, row.offset, [[T, EPT], [0, H], [1, HALF]])
                                   ).then_inc(gate_in[m % RING], 16)

                def lower(m, upper_parts, parts, c, lowered):
                    pool.wait_ge(upper_parts, sec.value("up", m + 1))
                    pool.tensor_tensor(parts[:, 2 + m % 2, :], expert_sb[:, m % RING, c:c + C],
                                       f(parts[:, m % 2, :]), ALU.subtract).then_inc(lowered, 1)

                for s in sec.steps:
                    if s[0] == "logits":
                        hold(acc_read, "acc", 0)
                        for m in range(RING):
                            load_expert(m)
                    if s[0] == "inputs":
                        pool.wait_ge(acts_hi, sec.value("acts", sec.no["acts"][s]))
                        pool.tensor_tensor(act_lo[:, :, :], xn[:, :, :], f(act_hi[:, :, :]),
                                           ALU.subtract).then_inc(acts_lo, 1)
                    if s[0] == "turn":
                        for m in range(2):
                            lower(m, keys_up, keys_parts, 0, keys_down)
                        hold(gates_out, "turn", sec.no["turn"][s], 16 * TT)
                        for m in range(RING):
                            load_gates(m)
                    if s[0] == "up":
                        m = s[1] * ET + s[2]
                        if m + 2 < NH * ET:
                            lower(m + 2, keys_up, keys_parts, 0, keys_down)
                        lower(m, vals_up, vals_parts, C, vals_down)
                        if m + RING < NH * ET:
                            hold(vals_down, "up", m + 1)
                            load_expert(m + RING)
                        if 1 <= m and m - 1 + RING < NH * ET:
                            b, n = sec.bank(("up",) + divmod(m - 1, ET))
                            hold(bank_read[b], b, n)
                            load_gates(m - 1 + RING)

            run(pool, emit)

        @block.tensor
        def _(pe):
            def split(acc, lhs, rhs, start, stop):
                (lh, ll), (rh, rl) = lhs, rhs
                pe.matmul(acc, lh, rh, start=start, stop=False)
                pe.matmul(acc, lh, rl, start=False, stop=False)
                return pe.matmul(acc, ll, rh, start=False, stop=stop)

            def parts(m, k, lo, hi):
                return w_hi[:, m, k, lo:hi], w_lo[:, m, k, lo:hi]

            def expert(both, m, n):
                return both[:, m % 2, P * n:P * n + P], both[:, 2 + m % 2, P * n:P * n + P]

            def acts(k, lo, hi):
                return act_hi[:, k, lo:hi], act_lo[:, k, lo:hi]

            def emit(sec, it):
                def bank(u):
                    b, n = sec.bank(u)
                    if sec.any(b, n - 1):
                        pe.wait_ge(bank_read[b], sec.value(b, n - 1))
                    return (ps_one if b[:3] == "one" else ps_two)[:, int(b[3]), :]

                def filled(mm, u):
                    mm.then_inc(bank_full[sec.bank(u)[0]], 1)

                def read(u):
                    b, n = sec.bank(u)
                    pe.wait_ge(bank_read[b], sec.value(b, n))

                def maxima(s):
                    _, st, g, j, hf = s
                    u = ("top", st, g, j, PH * hf + PH - 1)
                    others = [("top", st, g, j, i) for i in range(PH * hf, PH * hf + PH - 1)]
                    others = [o for o in others if sec.bank(o)[0] != sec.bank(u)[0]]
                    return others[-1:] + [u]

                def times_values(s):
                    _, st, g, hf, k, wide = s
                    a = first(st, hf, k)
                    n = 2 if wide else G
                    read(s + (n - 2,))
                    read(s + (n - 1,))
                    if k == 0:
                        if g == 0:
                            pe.wait_ge(v_ready, sec.value("v", sec.no["v"][("v", st, (last_tile(st, hf) - 1) // 2)]))
                        if sec.any("acc", sec.no["acc"][("norm", st, g, hf)] - 1):
                            pe.wait_ge(acc_read, sec.value("acc", sec.no["acc"][("norm", st, g, hf)] - 1))
                        if sec.any("norm", sec.no["norm"][("norm", st, g, hf)] - 1):
                            pe.wait_ge(out_read, sec.value("norm", sec.no["norm"][("norm", st, g, hf)] - 1))
                    for j in range(G):
                        c = P * g + HD * j
                        pe.matmul(ps_acc[HD * j:HD * j + HD, 0, a:HALF], v_sb[:, k, c:c + HD],
                                  probs[:, sec.no["mix"][s] % 2, j, a:HALF],
                                  start=(k == 0), stop=(k == last_tile(st, hf)))

                def sums(s):
                    _, st, g, hf, k, _ = s
                    a = first(st, hf, k)
                    for j in range(G):
                        mm = pe.matmul(ps_acc[HD * j:HD * j + HD, 1, a:HALF], ones32[:],
                                       probs[:, sec.no["mix"][s] % 2, j, a:HALF],
                                       start=(k == 0), stop=(k == last_tile(st, hf)))
                    mm.then_inc(mixed, 1)

                def times_down(hf, j):
                    m = hf * ET + j
                    pe.wait_ge(gated_down, sec.value("up", m + 1))
                    pe.wait_ge(vals_down, sec.value("up", m + 1))
                    if j == 0:
                        pe.wait_ge(acc_read, sec.value("acc", sec.no["acc"][("down", hf)] - 1))
                    for ct in range(CT):
                        mm = split(ps_acc[:, ct, :], expert(vals_parts, m, ct),
                                   (gated_hi[:, m % 2, :], gated_lo[:, m % 2, :]), j == 0, j == ET - 1)
                    mm.then_inc(downed, 1)

                for s in sec.steps:
                    kind = s[0]
                    if kind == "gn":
                        pe.wait_ge(gn_stats, sec.value("gn", sec.no["gn"][s]))
                        filled(pe.matmul(bank(s)[:, 0:2 * CT], block_w[:],
                                         small[:, 0, :, :].rearrange("p k s -> p (k s)"),
                                         start=True, stop=True), s)
                    elif kind == "qk":
                        _, st, g, w, hf = s
                        key = ("parts", hf) if st else ("split", hf)
                        if g == 0:
                            pe.wait_ge(acts_lo, sec.value("acts", sec.no["acts"][key]))
                        acc = bank(s)
                        m = 4 * st + "qk".index(w)
                        for k in range(CT):
                            mm = split(acc, parts(m, k, P * g, P * g + P),
                                       acts(k, HALF * hf, HALF * hf + HALF), k == 0, k == CT - 1)
                        filled(mm, s)
                    elif kind == "v":
                        _, st, n = s
                        acc = bank(s)
                        for i in range(2):
                            at = (2 * n + i) * P
                            for k in range(CT):
                                mm = split(acc[:, C * i:C * i + C], acts(k, at, at + P),
                                           parts(4 * st + 2, k, 0, C), k == 0, k == CT - 1)
                        filled(mm, s)
                    elif kind == "top":
                        _, st, g, j, i = s
                        if i % PH == 0:
                            for hf in [i // PH] if st else range(NH) if i == 0 else []:
                                n = sec.no[f"stacks{g}{hf}"][("stack", st, g)] if st or g else 0
                                pe.wait_ge(stacked[g][hf][j], sec.value(f"stacks{g}{hf}", n, STACK))
                        acc = bank(s)
                        n_keys = cols(st, i)
                        for c0 in range(0, n_keys, HALF):
                            c1 = min(c0 + HALF, n_keys)
                            diag = st == 1 and c1 == n_keys
                            mm = pe.matmul(acc[:, c0:c1], q_st[0:MID, g, j, P * i:P * i + P],
                                           k_st[0:MID, g, j, c0:c1], start=True, stop=not diag)
                            if diag:
                                mm = pe.matmul(acc[:, c1 - P:c1], ident_bf[:], mask_qk[:], start=False, stop=True)
                        filled(mm, s)
                    elif kind == "row":
                        _, st, g, j, hf = s
                        for u in maxima(s):
                            if sec.bank(u)[0] != sec.bank(s)[0]:
                                read(u)
                        acc = bank(s)
                        for i in range(PH * hf, PH * hf + PH):
                            mm = pe.matmul(acc[MID:MID + 1, P * i:P * i + P], tops[:, j, i:i + 1], minus_bf[:],
                                           start=True, stop=True)
                        filled(mm, s)
                    elif kind == "mix":
                        _, st, g, hf, k, wide = s
                        if k == 0:
                            pe.wait_ge(row_ready, sec.value("row", sec.no["row"][("row", st, g, G - 1, hf)]))
                        a = first(st, hf, k)
                        diag = st == 1 and k >= PH * hf
                        per = 2 if wide else 1
                        for n in range(G // per):
                            if n == G // per // 2 and k > 0:
                                times_values(("mix", st, g, hf, k - 1, wide))
                            u = s + (n,)
                            acc = bank(u)
                            for j in range(per * n, per * n + per):
                                at = acc[:, HALF * (j % per):HALF * (j % per) + HALF]
                                mm = pe.matmul(at[:, a:HALF], k_st[0:MID + 1, g, j, P * k:P * k + P],
                                               q_st[0:MID + 1, g, j, HALF * hf + a:HALF * hf + HALF],
                                               start=True, stop=not diag)
                                if diag:
                                    mm = pe.matmul(at[:, a:a + P], ident_bf[:], mask_kq[:], start=False, stop=True)
                            filled(mm, u)
                        if k > 0:
                            sums(("mix", st, g, hf, k - 1, wide))
                    elif kind == "norm":
                        _, st, g, hf = s
                        times_values(last_mix(sec, s))
                        sums(last_mix(sec, s))
                    elif kind == "out":
                        _, st, hf, ct = s
                        pe.wait_ge(att_lo, sec.value("fin", sec.no["fin"][("fin", st, CT - 1, hf)]))
                        acc = bank(s)
                        for k in range(CT):
                            mm = split(acc, parts(4 * st + 3, k, P * ct, P * ct + P),
                                       acts(k, HALF * hf, HALF * hf + HALF), k == 0, k == CT - 1)
                        filled(mm, s)
                    elif kind == "lna":
                        _, ln, hf = s
                        for ct in range(CT):
                            read(("out", ln, hf, ct))
                        acc = bank(s)
                        for k in range(CT):
                            mm = pe.matmul(acc, mean_w[:], x_res[:, k, half(hf)], start=(k == 0), stop=(k == CT - 1))
                        filled(mm, s)
                    elif kind == "lnb":
                        pe.wait_ge(squared, sec.value("lnb", sec.no["lnb"][s]))
                        acc = bank(s)
                        for k in range(CT):
                            mm = pe.matmul(acc, mean_w[:], squares[:, k, :], start=(k == 0), stop=(k == CT - 1))
                        filled(mm, s)
                    elif kind == "logits":
                        pe.wait_ge(xn_ready, sec.value("lnb", 0))
                        acc = bank(s)
                        for i in range(TT):
                            for k in range(CT):
                                mm = pe.matmul(acc[:, E * i:E * i + E], xn[:, k, P * i:P * i + P], sel_w[:, k, :],
                                               start=(k == 0), stop=(k == CT - 1))
                        filled(mm, s)
                    elif kind == "turn":
                        pe.wait_ge(gates, sec.value("logits", 1))
                        acc = bank(s)
                        for hf in range(NH):
                            mm = pe.transpose(acc[:, P * hf:P * hf + P],
                                              squares[:, 0, P * hf:P * hf + P],
                                              ident[:])
                        filled(mm, s)
                    elif kind == "up":
                        _, hf, j = s
                        m = hf * ET + j
                        if m == 0:
                            pe.wait_ge(acts_lo, sec.value("acts", sec.no["acts"][("inputs",)]))
                        pe.wait_ge(keys_down, sec.value("up", m + 1))
                        acc = bank(s)
                        for k in range(CT):
                            mm = split(acc, expert(keys_parts, m, k), acts(k, HALF * hf, HALF * hf + HALF),
                                       k == 0, k == CT - 1)
                        filled(mm, s)
                        if j > 1:
                            times_down(hf, j - 2)
                    elif kind == "down":
                        times_down(s[1], ET - 2)
                        times_down(s[1], ET - 1)

            pe.wait_ge(consts, N_CONSTS)
            pe.wait_ge(fills, 2)
            pe.wait_ge(weights_hi, 1)
            pe.wait_ge(weights_lo, 1)
            run(pe, emit)

        @block.scalar
        def _(act):
            act.preload_act_table_set("natural_log_exp_and_others")
            staged = probs[:, :, :, :].rearrange("p a g t -> p (a g t)")
            act.wait_ge(weights_in, 64)
            act.copy(w_hi[:, :, :, :].rearrange("p m k c -> p (m k c)"), staged).then_inc(weights_hi, 1)
            act.wait_ge(weights_lo, 1)

            def emit(sec, it):
                def full(u):
                    b, n = sec.bank(u)
                    act.wait_ge(bank_full[b], sec.value(b, n))
                    return (ps_one if b[:3] == "one" else ps_two)[:, int(b[3]), :]

                def read(u):
                    b, n = sec.bank(u)
                    act.wait_ge(bank_read[b], sec.value(b, n))

                def done(ins, u):
                    ins.then_inc(bank_read[sec.bank(u)[0]], 1)

                def logarithms():
                    return sec.value("gn", gn_seen) + sec.value("lnb", lnb_seen) + sec.value("div", div_seen)

                def inverse_root(out_, var, ready):
                    act.activation(out_, var, ACT.Ln).then_inc(logged, 1)
                    act.wait_ge(logged, logarithms())
                    act.activation(out_, out_, ACT.Exp, scale=-0.5).then_inc(ready, 1)

                def upper_keys(m):
                    r = m % RING
                    act.wait_ge(expert_in[r], (sec.value("turn", 0) * (NH * ET // RING) + m // RING + 1) * 16)
                    act.copy(keys_parts[:, m % 2, :], expert_sb[:, r, 0:C]).then_inc(keys_up, 1)

                gn_seen = lnb_seen = div_seen = 0
                for s in sec.steps:
                    kind = s[0]
                    if kind == "gn":
                        gn_seen += 1
                        act.wait_ge(gn_var, sec.value("gn", gn_seen))
                        inverse_root(small[:, 5, :, 0], small[:, 4, :, 0], gn_root)
                    elif kind == "split":
                        hf = s[1]
                        act.wait_ge(xt_ready, sec.value("split", sec.no["split"][s]))
                        if sec.name != "first":
                            read(("out", 1, hf, CT - 1))
                        act.copy(act_hi[:, :, half(hf)], xt[:, :, :]).then_inc(acts_hi, 1)
                    elif kind == "qk":
                        _, st, g, w, hf = s
                        acc = full(s)
                        if w == "q":
                            other = 1 - g
                            n = {(0, 0): 2, (0, 1): 0, (1, 0): 1, (1, 1): 1}[(st, g)] if sec.name != "first" else 0
                            for j in range(G):
                                if sec.any(f"stacks{other}{hf}", n):
                                    act.wait_ge(stacked[other][hf][j], sec.value(f"stacks{other}{hf}", n, STACK))
                        m = 4 * st + "qk".index(w)
                        act.activation(nat[:, 2 * "qk".index(w), half(hf)], acc, ACT.Identity,
                                       bias=bias[:, m, g:g + 1]).then_inc(nat_hi_ready, 1)
                    elif kind == "v":
                        _, st, n = s
                        done(act.copy(v_sb[:, 2 * n:2 * n + 2, :].rearrange("p i c -> p (i c)"), full(s)), s)
                        b, number = sec.bank(s)
                        act.wait_ge(bank_read[b], sec.value(b, number))
                        act.sem_inc(v_ready, 1)
                    elif kind == "row":
                        _, st, g, j, hf = s
                        b, n = sec.bank(s)
                        full(s)
                        done(act.copy(q_st[MID:MID + 1, g, j, half(hf)],
                                      ps_two[MID:MID + 1, int(b[3]), half(hf)]), s)
                        act.wait_ge(bank_read[b], sec.value(b, n))
                        act.sem_inc(row_ready, 1)
                    elif kind == "mix":
                        _, st, g, hf, k, wide = s
                        a = first(st, hf, k)
                        n = sec.no["mix"][s]
                        if sec.any("mix", n - 2):
                            act.wait_ge(mixed, sec.value("mix", n - 2))
                        if n <= 2 and sec.name == "body":
                            act.wait_ge(acc_read, sec.value("acc", sec.no["acc"][("down", NH - 1)]))
                        per = 2 if wide else 1
                        for i in range(G // per):
                            acc = full(s + (i,)).rearrange("p (g t) -> p g t", g=per)
                            done(act.activation(probs[:, n % 2, per * i:per * i + per, a:HALF], acc[:, :, a:HALF],
                                                ACT.Exp, scale=SCALE), s + (i,))
                    elif kind == "norm":
                        _, st, g, hf = s
                        act.wait_ge(mixed, sec.value("mix", sec.no["mix"][last_mix(sec, s)]))
                        if sec.any("norm", sec.no["norm"][s] - 1):
                            act.wait_ge(att_ready, sec.value("div", sec.no["norm"][s] - 1))
                        act.copy(o_sb[:], ps_acc[:, 0, :]).then_inc(out_read, 1)
                    elif kind == "div":
                        _, st, g, hf = s
                        if sec.any("lnb", lnb_seen):
                            act.wait_ge(xn_ready, sec.value("lnb", lnb_seen))
                        div_seen += 1
                        act.wait_ge(acc_read, sec.value("acc", sec.no["acc"][("norm",) + s[1:]]))
                        act.activation(rstd[:], rsum[:], ACT.Ln).then_inc(logged, 1)
                        act.wait_ge(logged, logarithms())
                        act.activation(rstd[:], rstd[:], ACT.Exp, scale=-1.0).then_inc(inverse, 1)
                    elif kind == "fin":
                        _, st, g, hf = s
                        act.wait_ge(att_ready, sec.value("div", sec.no["norm"][("norm",) + s[1:]]))
                        act.activation(act_hi[:, g, half(hf)], rsum[:], ACT.Identity,
                                       bias=bias[:, 4 * st + 2, g:g + 1]).then_inc(att_hi, 1)
                    elif kind == "lna":
                        _, ln, hf = s
                        read(s)
                        if sec.any("lnb", lnb_seen):
                            act.wait_ge(squared_read, sec.value("lnb", lnb_seen))
                        act.activation(squares[:, :, :], xn[:, :, half(hf)], ACT.Square).then_inc(squared, 1)
                    elif kind == "lnb":
                        _, ln, hf = s
                        lnb_seen += 1
                        read(s)
                        if sec.any("lnb", lnb_seen - 1):
                            act.wait_ge(xn_ready, sec.value("lnb", lnb_seen - 1))
                        act.wait_ge(att_ready, sec.value("div", div_seen))
                        inverse_root(rstd[:], var_sb[:], ln_root)
                    elif kind == "parts":
                        hf = s[1]
                        act.wait_ge(xn_ready, sec.value("lnb", sec.no["lnb"][("lnb", 0, hf)]))
                        act.copy(act_hi[:, :, half(hf)], xn[:, :, half(hf)]).then_inc(acts_hi, 1)
                    elif kind == "inputs":
                        read(("qk", 0, 1, "k", 1) if sec.name == "body" else ("logits",))
                        act.wait_ge(xn_ready, sec.value("lnb", 0))
                        act.copy(act_hi[:, :, :], xn[:, :, :]).then_inc(acts_hi, 1)
                    elif kind == "turn":
                        for g in range(CT):
                            for hf in range(NH):
                                for j in range(G):
                                    n = g if sec.name == "body" else 0
                                    act.wait_ge(stacked[g][hf][j], sec.value(f"stacks{g}{hf}", n, STACK))
                        for m in range(2):
                            upper_keys(m)
                    elif kind == "up":
                        _, hf, j = s
                        m = hf * ET + j
                        read(s)
                        if m + 2 < NH * ET:
                            upper_keys(m + 2)
                        if m >= 2:
                            act.wait_ge(downed, sec.value("up", m - 1))
                        act.copy(gated_hi[:, m % 2, :], gated[:, m % RING, :]).then_inc(gated_up, 1)
                        act.copy(vals_parts[:, m % 2, :], expert_sb[:, m % RING, C:2 * C]).then_inc(vals_up, 1)
                    elif kind == "logits":
                        done(act.activation(w_tok, full(s)[:, 0:TT * E].rearrange("p (i e) -> p i e", e=E),
                                            ACT.Exp, scale=-1.0), s)

            run(act, emit)

        @block.vector
        def _(dve):
            staged = probs[:, :, :, :].rearrange("p a g t -> p (a g t)")
            dve.memset(f(k_st[MID:MID + 1, :, :, :]), 1.0).then_inc(fills, 1)
            dve.memset(pad_sel[:], -1.0).then_inc(fills, 1)
            dve.wait_ge(weights_hi, 1)
            dve.wait_ge(weights_in, 64)
            dve.tensor_tensor(w_lo[:, :, :, :].rearrange("p m k c -> p (m k c)"), staged,
                              f(w_hi[:, :, :, :].rearrange("p m k c -> p (m k c)")),
                              ALU.subtract).then_inc(weights_lo, 1)
            dve.wait_ge(consts, N_CONSTS)
            dve.wait_ge(weights_lo, 1)
            dve.wait_ge(fills, 2)

            def emit(sec, it):
                def full(u):
                    b, n = sec.bank(u)
                    dve.wait_ge(bank_full[b], sec.value(b, n))
                    return (ps_one if b[:3] == "one" else ps_two)[:, int(b[3]), :]

                def read(u):
                    b, n = sec.bank(u)
                    dve.wait_ge(bank_read[b], sec.value(b, n))

                def done(ins, u):
                    ins.then_inc(bank_read[sec.bank(u)[0]], 1)

                def lower(m):
                    dve.wait_ge(gated_up, sec.value("up", m + 1))
                    dve.tensor_tensor(gated_lo[:, m % 2, :], gated[:, m % RING, :], f(gated_hi[:, m % 2, :]),
                                      ALU.subtract).then_inc(gated_down, 1)

                links = [0]

                def link(ins):
                    links[0] += 1
                    ins.then_inc(linked, 1)
                    dve.wait_ge(linked, sec.value("link", links[0]))

                def refine(y, var, tmp):
                    link(dve.tensor_tensor(tmp, var, y, ALU.mult))
                    link(dve.tensor_tensor(tmp, tmp, y, ALU.mult))
                    link(dve.tensor_scalar(tmp, tmp, -0.5, 1.5, ALU.mult, ALU.add))
                    link(dve.tensor_tensor(y, y, tmp, ALU.mult))

                for s in sec.steps:
                    kind = s[0]
                    if kind == "stats":
                        dve.wait_ge(x_loaded, sec.value("stats", 1, 16))
                        for k in range(CT):
                            for hf in range(NH):
                                ins = dve.bn_stats(st6[:, k, hf, :], x_in[:, k, half(hf)])
                        link(ins)
                        dve.sem_inc(passed, 1)
                        for k in range(CT):
                            ins = dve.bn_aggr(mv[:, k, :], st6[:, k, :, :].rearrange("p h s -> p (h s)"))
                        link(ins)
                        dve.tensor_copy(small[:, 0, :, 0], mv[:, :, 0])
                        link(dve.tensor_tensor(small[:, 1, :, 0], mv[:, :, 0], mv[:, :, 0], ALU.mult))
                        dve.tensor_tensor(small[:, 0, :, 1], small[:, 1, :, 0], mv[:, :, 1],
                                          ALU.add).then_inc(gn_stats, 1)
                    elif kind == "gn":
                        n = sec.no["gn"][s]
                        acc = full(s)
                        done(dve.tensor_copy(small[:, 2, :, :].rearrange("p k s -> p (k s)"), acc[:, 0:2 * CT]), s)
                        read(s)
                        link(dve.tensor_tensor(small[:, 3, :, 0], small[:, 2, :, 0], small[:, 2, :, 0], ALU.mult))
                        link(dve.tensor_tensor(small[:, 3, :, 1], small[:, 2, :, 1], small[:, 3, :, 0],
                                               ALU.subtract))
                        dve.tensor_scalar(small[:, 4, :, 0], small[:, 3, :, 1], 1e-5, None,
                                          ALU.add).then_inc(gn_var, 1)
                        dve.wait_ge(gn_root, sec.value("gn", n))
                        refine(small[:, 5, :, 0], small[:, 4, :, 0], small[:, 5, :, 1])
                        link(dve.tensor_tensor(small[:, 6, :, 0], small[:, 5, :, 0], gnw[:, 0, :], ALU.mult))
                        dve.tensor_tensor(small[:, 6, :, 1], small[:, 2, :, 0], small[:, 6, :, 0],
                                          ALU.mult).then_inc(linked, 1)
                        links[0] += 1
                        dve.wait_ge(linked, sec.value("link", links[0]))
                        dve.tensor_tensor(small[:, 7, :, 0], gnw[:, 1, :], small[:, 6, :, 1],
                                          ALU.subtract).then_inc(offsets, 1)
                        dve.wait_ge(offsets, sec.value("gn", n))
                    elif kind == "split":
                        hf = s[1]
                        n = sec.no["split"][s]
                        if sec.any("acts", sec.no["acts"][s] - 1):
                            dve.wait_ge(acts_lo, sec.value("acts", sec.no["acts"][s] - 1))
                        for k in range(CT):
                            ins = dve.tensor_scalar(xt[:, k, :], x_in[:, k, half(hf)], small[:, 6, k, 0:1],
                                                    small[:, 7, k, 0:1], ALU.mult, ALU.add)
                        ins.then_inc(xt_ready, 1)
                        dve.wait_ge(xt_ready, sec.value("split", n))
                        dve.wait_ge(acts_hi, sec.value("acts", sec.no["acts"][s]))
                        dve.tensor_tensor(act_lo[:, :, half(hf)], xt[:, :, :], f(act_hi[:, :, half(hf)]),
                                          ALU.subtract).then_inc(acts_lo, 1)
                    elif kind == "qk":
                        _, st, g, w, hf = s
                        m, n = 4 * st + "qk".index(w), 2 * "qk".index(w)
                        acc = full(s)
                        dve.wait_ge(nat_hi_ready, sec.value("qk", sec.no["qk"][s]))
                        done(dve.scalar_tensor_tensor(out=nat[:, n + 1, half(hf)], in0=acc, scalar=bias[:, m, g:g + 1],
                                                      in1=f(nat[:, n, half(hf)]), op0=ALU.add,
                                                      op1=ALU.subtract), s)
                    elif kind == "top":
                        _, st, g, j, i = s
                        acc = full(s)
                        if i % PH == 0:
                            if sec.any("row", sec.no["row"][("row", st, g, j, i // PH)] - G):
                                dve.wait_ge(row_ready, sec.value("row", sec.no["row"][("row", st, g, j, i // PH)] - G))
                        done(dve.reduce_max(tops[:, j, i:i + 1], acc[:, 0:cols(st, i)], AX_X), s)
                    elif kind == "norm":
                        _, st, g, hf = s
                        dve.wait_ge(mixed, sec.value("mix", sec.no["mix"][last_mix(sec, s)]))
                        if sec.any("fin", sec.no["norm"][s] - 1):
                            dve.wait_ge(att_lo, sec.value("fin", sec.no["norm"][s] - 1))
                        dve.tensor_copy(rsum[:], ps_acc[:, 1, :]).then_inc(acc_read, 1)
                    elif kind == "div":
                        _, st, g, hf = s
                        dve.wait_ge(inverse, sec.value("div", sec.no["div"][s]))
                        link(dve.tensor_tensor(rsum[:], rsum[:], rstd[:], ALU.mult))
                        link(dve.scalar_tensor_tensor(out=rsum[:], in0=rsum[:], scalar=-2.0, in1=rstd[:],
                                                      op0=ALU.add, op1=ALU.mult))
                        dve.wait_ge(out_read, sec.value("div", sec.no["div"][s]))
                        dve.scalar_tensor_tensor(out=rsum[:], in0=o_sb[:], scalar=-1.0, in1=rsum[:],
                                                 op0=ALU.mult, op1=ALU.mult).then_inc(att_ready, 1)
                    elif kind == "fin":
                        _, st, g, hf = s
                        n = sec.no["fin"][s]
                        dve.wait_ge(att_ready, sec.value("div", n))
                        dve.wait_ge(att_hi, sec.value("fin", n))
                        dve.scalar_tensor_tensor(out=act_lo[:, g, half(hf)], in0=rsum[:],
                                                 scalar=bias[:, 4 * st + 2, g:g + 1],
                                                 in1=f(act_hi[:, g, half(hf)]),
                                                 op0=ALU.add, op1=ALU.subtract).then_inc(att_lo, 1)
                    elif kind == "out":
                        _, st, hf, ct = s
                        acc = full(s)
                        before = x_res if st else x_in
                        if st == 0 and sec.name == "body":
                            dve.wait_ge(stored[hf], sec.value("turn", 1, 16))
                        done(dve.scalar_tensor_tensor(out=x_res[:, ct, half(hf)], in0=acc,
                                                      scalar=bias[:, 4 * st + 3, ct:ct + 1],
                                                      in1=before[:, ct, half(hf)], op0=ALU.add, op1=ALU.add), s)
                    elif kind == "lna":
                        _, ln, hf = s
                        acc = full(s)
                        for ct in range(CT):
                            read(("out", ln, hf, ct))
                        link(dve.tensor_tensor(xn[:, 0, half(hf)], x_res[:, 0, half(hf)], acc, ALU.subtract))
                        done(dve.tensor_tensor(xn[:, 1, half(hf)], x_res[:, 1, half(hf)], acc, ALU.subtract), s)
                    elif kind == "lnb":
                        _, ln, hf = s
                        acc = full(s)
                        done(dve.tensor_scalar(var_sb[:], acc, 1e-5, None, ALU.add), s)
                        read(s)
                        n = sec.no["lnb"][s]
                        dve.wait_ge(ln_root, sec.value("lnb", n))
                        refine(rstd[:], var_sb[:], rtmp)
                        dve.sem_inc(squared_read, 1)
                        link(dve.tensor_tensor(xn[:, 0, half(hf)], xn[:, 0, half(hf)], rstd[:], ALU.mult))
                        dve.tensor_tensor(xn[:, 1, half(hf)], xn[:, 1, half(hf)], rstd[:],
                                          ALU.mult).then_inc(xn_ready, 1)
                    elif kind == "parts":
                        hf = s[1]
                        dve.wait_ge(xn_ready, sec.value("lnb", sec.no["lnb"][("lnb", 0, hf)]))
                        dve.wait_ge(acts_hi, sec.value("acts", sec.no["acts"][s]))
                        dve.tensor_tensor(act_lo[:, :, half(hf)], xn[:, :, half(hf)], f(act_hi[:, :, half(hf)]),
                                          ALU.subtract).then_inc(acts_lo, 1)
                    elif kind == "logits":
                        read(s)
                        link(dve.tensor_scalar(w_tok, w_tok, 1.0, None, ALU.add))
                        link(dve.reciprocal(pad_sel[:, :, 0:E], w_tok))
                        dve.sem_inc(passed, 1)
                        for i in range(TT):
                            ins = dve.max(top8[:, i, :], pad_sel[:, i, 0:E])
                        link(ins)
                        link(dve.memset(top8[:, :, 2:8], -1.0))
                        dve.sem_inc(passed, 1)
                        for i in range(TT):
                            ins = dve.match_replace(rest[:, i, :], top8[:, i, :], pad_sel[:, i, :], 0.0)
                        link(ins)
                        dve.tensor_tensor(w_tok, pad_sel[:, :, 0:E], rest[:, :, 0:E],
                                          ALU.subtract).then_inc(gates, 1)
                    elif kind == "turn":
                        done(dve.tensor_copy(w_turn[:].rearrange("p h t -> p (h t)"), full(s)[:, 0:NH * P]), s)
                    elif kind == "up":
                        _, hf, j = s
                        m = hf * ET + j
                        acc = full(s)
                        r = m % RING
                        dve.wait_ge(gate_in[r], (sec.value("turn", 0) * (NH * ET // RING) + m // RING + 1) * 16)
                        if m >= RING:
                            dve.wait_ge(gated_down, sec.value("up", m + 1 - RING))
                        done(dve.scalar_tensor_tensor(out=gated[:, r, :], in0=acc, scalar=0.0,
                                                      in1=gate_bc[:, r, :], op0=ALU.max, op1=ALU.mult), s)
                        if j:
                            lower(m - 1)
                    elif kind == "lower":
                        lower((s[1] + 1) * ET - 1)
                    elif kind == "down":
                        hf = s[1]
                        dve.wait_ge(downed, sec.value("up", (hf + 1) * ET))
                        dve.tensor_tensor(x_res[:, 0, half(hf)], ps_acc[:, 0, :], x_res[:, 0, half(hf)], ALU.add)
                        dve.tensor_tensor(x_res[:, 1, half(hf)], ps_acc[:, 1, :], x_res[:, 1, half(hf)],
                                          ALU.add).then_inc(acc_read, 1)
                assert links[0] == len(sec.no.get("link", {})), (sec.name, links[0])

            run(dve, emit)


def next_batch(it, batches):
    return it + 1 if isinstance(it, int) else (it + 1) % batches


def kernel(**inputs):
    import concourse.bacc as bacc
    from concourse.bass_utils import run_bass_kernel_spmd

    a = {n: np.asarray(v) for n, v in inputs.items()}
    B, C, Hh, Ww = a["x"].shape
    T = Hh * Ww
    CT = C // P
    heads = 8
    ch = C // heads
    qkv = a["L0_conv_qkv_w"].reshape(heads, 3, ch, C)
    qkv_b = a["L0_conv_qkv_b"].reshape(heads, 3, ch)
    mats = [qkv[:, n].reshape(C, C).T for n in range(3)] + [a["L0_conv_proj_w"].T]
    mats += [a["L1_attn_W_" + n] for n in "QKVO"]
    vecs = [qkv_b[:, n].reshape(C) for n in range(3)] + [a["L0_conv_proj_b"]]
    vecs += [a["L1_attn_b_" + n] for n in "QKVO"]
    keys = a["L1_ffn_keys"]
    E, _, H = keys.shape
    ET = E * H // P

    def by_partition(m):
        return np.moveaxis(m.reshape(m.shape[:-1] + (CT, P)), -1, 0)

    arrays = {
        "x_in_dram": a["x"].reshape(B, C, T),
        "mats_dram": np.stack(mats).reshape(8, CT, P, C).transpose(2, 0, 1, 3),
        "vecs_dram": by_partition(np.stack(vecs)),
        "norm_dram": by_partition(np.stack([a["L0_conv_norm_w"], a["L0_conv_norm_b"]])),
        "sel_dram": a["L1_ffn_expert_sel"].T.reshape(CT, P, E).transpose(1, 0, 2),
        "experts_dram": np.concatenate(
            [keys.transpose(1, 0, 2).reshape(CT, P, ET, P).transpose(2, 1, 0, 3).reshape(ET, P, C),
             a["L1_ffn_values"].reshape(ET, P, C)], axis=2),
    }
    arrays = {n: np.ascontiguousarray(v) for n, v in arrays.items()}
    nc = bacc.Bacc("TRN2", target_bir_lowering=False, num_devices=1)
    args = [nc.dram_tensor(n, v.shape, mybir.dt.from_np(v.dtype), kind="ExternalInput").ap()
            for n, v in arrays.items()]
    out = nc.dram_tensor("out_dram", (B, C, T), F32, kind="ExternalOutput").ap()
    w_dram = nc.dram_tensor("gates_dram", (E, T), F32, kind="Internal").ap()
    bass_hybrid_kernel(nc, *args, out, w_dram)
    r = run_bass_kernel_spmd(nc, [arrays], core_ids=[0])
    return r.results[0]["out_dram"].reshape(B, C, Hh, Ww)
```
